# Optimizing a Trainium2 kernel written in Bass

```python
import numpy as np
import jax
import jax.numpy as jnp

def _softmax(x, axis=-1):
    return jax.nn.softmax(x, axis=axis)

def _gelu(x):
    return jax.nn.gelu(x, approximate=True)

def _silu(x):
    return jax.nn.silu(x)

def _sigmoid(x):
    return jax.nn.sigmoid(x)

def _layernorm(x, axis=-1, eps=1e-05):
    m = jnp.mean(x, axis=axis, keepdims=True)
    v = jnp.var(x, axis=axis, keepdims=True)
    return (x - m) / jnp.sqrt(v + eps)

def _scatter_add(tgt, idx, src, axis=0):
    return tgt.at[idx].add(src)

def _segment_sum(src, seg, n):
    return jax.ops.segment_sum(src, seg, n)
kernel_name = 'mk_adaln_d1_jaxref_r8_7e01bd'

def setup_inputs(seed: int=0):
    np.random.seed(seed)
    _w = jnp.asarray

    def _L0_attn_setup():
        import jax, jax.numpy as jnp
        import numpy as np
        import math
        EMBED_DIM = 256
        NUM_HEADS = 16
        HEAD_DIM = EMBED_DIM // NUM_HEADS
        BATCH = 4
        SEQ = 256
        key = jax.random.key(seed)
        ks = jax.random.split(key, 5)
        scale_qkv = 1.0 / math.sqrt(EMBED_DIM)
        x = jax.random.normal(ks[0], (BATCH, SEQ, EMBED_DIM), dtype=jnp.float32)
        w_qkv = jax.random.normal(ks[1], (3 * EMBED_DIM, EMBED_DIM), dtype=jnp.float32) * scale_qkv
        b_qkv = jnp.zeros((3 * EMBED_DIM,), dtype=jnp.float32)
        w_o = jax.random.normal(ks[2], (EMBED_DIM, EMBED_DIM), dtype=jnp.float32) * scale_qkv
        b_o = jnp.zeros((EMBED_DIM,), dtype=jnp.float32)
        return {'x': x, 'w_qkv': w_qkv, 'b_qkv': b_qkv, 'w_o': w_o, 'b_o': b_o}
    _L0_attn_in = _L0_attn_setup()

    def _L0_ffn_setup():
        import jax, jax.numpy as jnp
        import numpy as np
        TOP_P = 0.9
        S, B, H, I, E = (256, 4, 256, 512, 8)

        def _top_p_weights(probs, top_p):
            order = jnp.argsort(-probs, axis=-1)
            sp = jnp.take_along_axis(probs, order, axis=-1)
            cum = jnp.cumsum(sp, axis=-1)
            exceed = cum > top_p
            first_idx = jnp.argmax(exceed, axis=-1)
            first = jnp.arange(probs.shape[-1])[None, :] == first_idx[:, None]
            keep = ~exceed | first
            kept = jnp.where(keep, sp, 0.0)
            t_idx = jnp.arange(probs.shape[0])[:, None]
            return jnp.zeros_like(probs).at[t_idx, order].set(kept)
        key = jax.random.key(seed)
        ks = jax.random.split(key, 5)
        scale = 0.02
        return {'hidden_states': jax.random.normal(ks[0], (S, B, H), dtype=jnp.float32), 'router_w': jax.random.normal(ks[1], (E, H), dtype=jnp.float32) * scale, 'gate_w': jax.random.normal(ks[2], (E, I, H), dtype=jnp.float32) * scale, 'up_w': jax.random.normal(ks[3], (E, I, H), dtype=jnp.float32) * scale, 'down_w': jax.random.normal(ks[4], (E, H, I), dtype=jnp.float32) * scale}
    _L0_ffn_in = _L0_ffn_setup()
    _L0_c = _w((lambda *s: np.random.randn(*s).astype(np.float32) * 0.05)(16, 256))
    _L0_wmod = _w((lambda *s: np.random.randn(*s).astype(np.float32) * 0.05)(256, 6 * 256) * 256 ** (-0.5))
    _d = {'L0_attn_x': _L0_attn_in['x'], 'L0_attn_w_qkv': _L0_attn_in['w_qkv'], 'L0_attn_b_qkv': _L0_attn_in['b_qkv'], 'L0_attn_w_o': _L0_attn_in['w_o'], 'L0_attn_b_o': _L0_attn_in['b_o'], 'L0_ffn_router_w': _L0_ffn_in['router_w'], 'L0_ffn_gate_w': _L0_ffn_in['gate_w'], 'L0_ffn_up_w': _L0_ffn_in['up_w'], 'L0_ffn_down_w': _L0_ffn_in['down_w'], 'L0_c': _L0_c, 'L0_wmod': _L0_wmod}
    _x0 = _d['L0_attn_x']
    _d['L0_attn_x'] = jax.random.normal(jax.random.fold_in(jax.random.key(seed), 1), (16, 256, 256), dtype=_x0.dtype)
    del _x0
    return _d

def reference(L0_attn_x, L0_attn_w_qkv, L0_attn_b_qkv, L0_attn_w_o, L0_attn_b_o, L0_ffn_router_w, L0_ffn_gate_w, L0_ffn_up_w, L0_ffn_down_w, L0_c, L0_wmod):

    def _L0_attn_ref(x, w_qkv, b_qkv, w_o, b_o):
        import jax, jax.numpy as jnp
        import numpy as np
        import math
        EMBED_DIM = 256
        NUM_HEADS = 16
        HEAD_DIM = EMBED_DIM // NUM_HEADS
        BATCH = 4
        SEQ = 256
        B, S, D = x.shape
        qkv = jnp.einsum('bsd,ed->bse', x, w_qkv) + b_qkv
        qkv = qkv.reshape(B, S, 3, NUM_HEADS, HEAD_DIM)
        qkv = jnp.transpose(qkv, (2, 0, 3, 1, 4))
        q, k, v = (qkv[0], qkv[1], qkv[2])
        scores = jnp.einsum('bhqd,bhkd->bhqk', q, k) / math.sqrt(HEAD_DIM)
        probs = jax.nn.softmax(scores, axis=-1)
        out = jnp.einsum('bhqk,bhkd->bhqd', probs, v)
        out = jnp.transpose(out, (0, 2, 1, 3)).reshape(B, S, D)
        return jnp.einsum('bsd,ed->bse', out, w_o) + b_o

    def _L0_ffn_ref(hidden_states, router_w, gate_w, up_w, down_w):
        import jax, jax.numpy as jnp
        import numpy as np
        TOP_P = 0.9
        S, B, H, I, E = (256, 4, 256, 512, 8)

        def _top_p_weights(probs, top_p):
            order = jnp.argsort(-probs, axis=-1)
            sp = jnp.take_along_axis(probs, order, axis=-1)
            cum = jnp.cumsum(sp, axis=-1)
            exceed = cum > top_p
            first_idx = jnp.argmax(exceed, axis=-1)
            first = jnp.arange(probs.shape[-1])[None, :] == first_idx[:, None]
            keep = ~exceed | first
            kept = jnp.where(keep, sp, 0.0)
            t_idx = jnp.arange(probs.shape[0])[:, None]
            return jnp.zeros_like(probs).at[t_idx, order].set(kept)
        s, b, h = hidden_states.shape
        x = hidden_states.reshape(-1, h)
        probs = jax.nn.softmax(x @ router_w.T, axis=-1)
        w = _top_p_weights(probs, TOP_P)
        out = jnp.zeros_like(x)
        n_exp = router_w.shape[0]
        for e in range(n_exp):
            g = jax.nn.silu(x @ gate_w[e].T)
            u = x @ up_w[e].T
            y = g * u @ down_w[e].T
            out = out + y * w[:, e:e + 1]
        return out.reshape(s, b, h)
    x = L0_attn_x
    mod = (_silu(L0_c) @ L0_wmod).reshape(L0_c.shape[0], 6, 1, -1)
    sa, ca, ga, sb, cb, gb = (mod[:, 0], mod[:, 1], mod[:, 2], mod[:, 3], mod[:, 4], mod[:, 5])
    ga = (2 * (ga >= 0) - 1) * jnp.maximum(jnp.abs(ga), 0.25)
    gb = (2 * (gb >= 0) - 1) * jnp.maximum(jnp.abs(gb), 0.25)
    h = _layernorm(x, axis=-1) * (1 + ca) + sa
    x = x + ga * _L0_attn_ref(h, L0_attn_w_qkv, L0_attn_b_qkv, L0_attn_w_o, L0_attn_b_o)
    h = _layernorm(x, axis=-1) * (1 + cb) + sb
    x = x + gb * _L0_ffn_ref(h, L0_ffn_router_w, L0_ffn_gate_w, L0_ffn_up_w, L0_ffn_down_w)
    return x

_drawn_inputs = setup_inputs


def setup_inputs(seed=0):
    import zlib

    import numpy as np

    out = dict(_drawn_inputs(seed))
    spreads = {'L0_attn_b_qkv': (0.0, 0.324), 'L0_attn_b_o': (0.0, 0.315)}
    factors = {'L0_ffn_router_w': 8.0, 'L0_ffn_gate_w': 8.0, 'L0_ffn_up_w': 8.0, 'L0_ffn_down_w': 8.0}
    for name, (base, spread) in spreads.items():
        noise = np.random.default_rng([zlib.crc32(name.encode()), seed]).standard_normal(out[name].shape)
        drawn = base * np.exp(spread * noise) if base else spread * noise
        out[name] = jnp.asarray(drawn.astype(out[name].dtype))
    for name, factor in factors.items():
        out[name] = (out[name] * factor).astype(out[name].dtype)
    return out
```

```python
from contextlib import ExitStack

import concourse.bass as bass
from concourse import mybir

F32 = mybir.dt.float32
F16 = mybir.dt.float16
ALU = mybir.AluOpType
ACT = mybir.ActivationFunctionType
AX = mybir.AxisListType

P = 128
B, S, D = 16, 256, 256
H, HD = 16, 16
E, I = 8, 512
KD = D // P
TT = S // P
NT = B * TT
PAIRS = H // 2
EPS = 1e-5
TOP_P = 0.9
GATE_MIN = 0.25

XS = 16.0
WS = 256.0
QS = XS / HD ** 0.5
SS = XS * XS
MAXK = 256.0
VW = 32
STACK = 3 * HD

TB = 512
NB = B * S // TB
BT = TB // P
IJ = I // P
GU_SCALE = XS * WS
WPIECE = 2 * KD * P
STAGED = 2 * KD * I + IJ * D


class Batch:

    def __init__(self, half, par):
        self.half, self.par = half, par
        self.n = 2 * half + par

    def at(self, d):
        p = self.par + d
        return Batch(self.half + p // 2, p % 2)

    @property
    def real(self):
        return not isinstance(self.n, int) or 0 <= self.n < B


def wait(engine, sem, value):
    if isinstance(value, int) and value <= 0:
        return
    engine.wait_ge(sem, value)


def adaln_block(nc, x, wqkv_t, bqkv_p, wo_t, b_o, router_t, gate_t, up_t, down_t, c_t, wmod, out):
    with ExitStack() as ctx:
        def sb(name, shape, dt=F32):
            return ctx.enter_context(nc.sbuf_tensor(name, shape, dt))

        def sem(name):
            return ctx.enter_context(nc.semaphore(name))

        bank = ctx.enter_context(nc.psum_tensor("bank", [P, 8, 512], F32))

        x1 = sb("x1", [P, NT, D])
        acc = sb("acc", [P, NT, D])
        h2h = sb("h2h", [P, KD, B * S], F16)
        h2l = sb("h2l", [P, KD, B * S], F16)
        wts = sb("wts", [P, NT, E])
        ident = sb("ident", [P, P])

        wq_h = sb("wq_h", [P, KD, 3 * D], F16)
        wq_l = sb("wq_l", [P, KD, 3 * D], F16)
        wo_h = sb("wo_h", [P, KD, D], F16)
        wo_l = sb("wo_l", [P, KD, D], F16)
        wr_h = sb("wr_h", [P, KD, E], F16)
        wr_l = sb("wr_l", [P, KD, E], F16)
        bias_p = sb("bias_p", [P, 6])
        bias_s = sb("bias_s", [P, 6])
        bo_bc = sb("bo_bc", [P, D])
        silu_c = sb("silu_c", [P, KD, B])
        tanh_c = sb("tanh_c", [P, KD, B])
        modv = sb("modv", [P, 4, KD, B])
        gate_r = sb("gate_r", [B, 2, D])
        gate_s = sb("gate_s", [B, 2, D])
        gate_m = sb("gate_m", [B, 2, D])
        earlier = sb("earlier", [P, E, E])
        halfpow = sb("halfpow", [P, TT])
        eps = sb("eps", [P, TT])

        qst = sb("qst", [P, 2, PAIRS, S], F16)
        kst = sb("kst", [P, 2, PAIRS, S], F16)
        vx = sb("vx", [P, 2, TT, H, VW])
        prob = sb("prob", [P, 2, 2, TT, S])
        bn1 = sb("bn1", [P, TT, 6])
        parts1 = sb("parts1", [P, TT, 4])
        mv1 = sb("mv1", [P, TT, 2])
        ve1 = sb("ve1", [P, TT])
        rs1 = sb("rs1", [P, TT])
        xn1 = sb("xn1", [P, TT, D])
        bn2 = sb("bn2", [P, TT, 6])
        parts2 = sb("parts2", [P, TT, 4])
        mv2 = sb("mv2", [P, TT, 2])
        ve2 = sb("ve2", [P, TT])
        rs2 = sb("rs2", [P, TT])
        xn2 = sb("xn2", [P, TT, D])
        hT = sb("hT", [P, KD, S])
        hh = sb("hh", [P, KD, S], F16)
        hl = sb("hl", [P, KD, S], F16)
        q32 = sb("q32", [P, KD, S])
        qh = sb("qh", [P, KD, S], F16)
        ql = sb("ql", [P, KD, S], F16)
        k32 = sb("k32", [P, KD, S])
        kh = sb("kh", [P, KD, S], F16)
        kl = sb("kl", [P, KD, S], F16)
        mx = sb("mx", [P, TT, 2, PAIRS])
        nm = sb("nm", [H, S], F16)
        au = sb("au", [P, 4, S])
        rec = sb("rec", [P, TT, H])
        at = sb("at", [P, TT, D])
        aT = sb("aT", [P, KD, S])
        ah = sb("ah", [P, KD, S], F16)
        al = sb("al", [P, KD, S], F16)
        ga_bc = sb("ga_bc", [P, D])
        proj = sb("proj", [P, TT, D])
        gated = sb("gated", [P, TT, D])
        h2T = sb("h2T", [P, KD, S])
        lmax = sb("lmax", [P, TT])
        lsh = sb("lsh", [P, TT, E])
        pexp = sb("pexp", [P, TT, E])
        psum_r = sb("psum_r", [P, TT])
        prec = sb("prec", [P, TT])
        rp = sb("rp", [P, TT, E])
        before = sb("before", [P, TT, E, E])
        ties = sb("ties", [P, TT, E, E])
        cum = sb("cum", [P, TT, E])

        staged = sb("staged", [P, STAGED])
        gu_h = sb("gu_h", [P, IJ, WPIECE], F16)
        gu_l = sb("gu_l", [P, IJ, WPIECE], F16)
        dn_h = sb("dn_h", [P, IJ, D], F16)
        dn_l = sb("dn_l", [P, IJ, D], F16)
        hid_h = qst[:, :, :, :].rearrange("p a b c -> p (a b c)").rearrange("p (h j n) -> p h j n", h=2, j=IJ)
        hid_l = kst[:, :, :, :].rearrange("p a b c -> p (a b c)").rearrange("p (h j n) -> p h j n", h=2, j=IJ)
        probv = prob[:, :, :, :, :].rearrange("p a b c d -> p (a b c d)")
        th = [probv[:, 0:TB], probv[:, TB:2 * TB]]
        sg = [probv[:, 2 * TB:3 * TB], probv[:, 3 * TB:4 * TB]]
        hf = [hT[:, :, :].rearrange("p k s -> p (k s)"), q32[:, :, :].rearrange("p k s -> p (k s)")]
        gb_bc = at

        accf = acc[:, :, :].rearrange("p t d -> p (t d)")
        o_mod, o_qkv = 0, KD * 6 * D
        o_wo = o_qkv + KD * 3 * D
        o_r = o_wo + KD * D
        o_c = o_r + KD * E
        wmod32 = accf[:, o_mod:o_qkv].rearrange("p (k n) -> p k n", k=KD)
        wq32 = accf[:, o_qkv:o_wo].rearrange("p (k n) -> p k n", k=KD)
        wo32 = accf[:, o_wo:o_r].rearrange("p (k n) -> p k n", k=KD)
        wr32 = accf[:, o_r:o_c].rearrange("p (k n) -> p k n", k=KD)
        c32 = accf[:, o_c:o_c + KD * B].rearrange("p (k n) -> p k n", k=KD)
        staged_gu = staged[:, 0:2 * KD * I].rearrange("p (g n) -> p g n", g=2 * KD)
        staged_dn = staged[:, 2 * KD * I:STAGED]

        q_d = nc.dram_tensor("q_scratch", [2, 2, D, S], F16, kind="Internal").ap()
        k_d = nc.dram_tensor("k_scratch", [2, 2, D, S], F16, kind="Internal").ap()
        gates_d = nc.dram_tensor("gates_scratch", [2, B, D], F32, kind="Internal").ap()

        names = """c_in wmod_in wqkv_in wo_in bias_in bo_in bias_s_ready ident_ready tanhc_ready siluc_ready mod_done
            modv_ready gr_ready gates_ready gates_out wsplit_h wsplit_l consts_ready pow_ready
            ga_in scr_written st1_ready halves1_ready parts1_ready mv1_ready ve1_ready rs1_ready xn1_ready t1_done hT_ready hh_ready hl_ready
            qp_done q32_ready qh_ready ql_ready kp_done k32_ready kh_ready kl_ready vp_done v_ready
            sc_done max_done nmt_done nm_ready scT_done exp_done pv_done au_ready tn_done rec_ready at_ready
            ta_done aT_ready ah_ready al_ready op_done proj_ready gated_ready x1_ready
            st2_ready halves2_ready parts2_ready mv2_ready ve2_ready rs2_ready xn2_ready t2_done h2T_ready h2h_ready h2l_ready
            rt_done lmax_ready lsh_ready pexp_ready rsum_ready prec_ready rp_ready before_ready ties_ready
            tied_ready joined_ready weighed_ready cum_ready w_ready
            gu_in dn_in wgu_h wgu_l wdn_h wdn_l gu_done th_ready sg_ready hf_ready hidh_ready hidl_ready
            y_done acc_ready gb_in fin_mul fin_add out_done""".split()
        s = {n: sem(n) for n in names}
        x_in = [sem(f"x_in{p}") for p in range(2)]
        stack_in = [sem(f"stack_in{p}") for p in range(2)]
        nm_in = [sem(f"nm_in{p}") for p in range(2)]

        def passes(w_hi, w_lo, a_hi, a_lo):
            return ((w_hi, a_hi), (w_hi, a_lo), (w_lo, a_hi))

        def run_stage_one(engine, iteration, between=()):
            for n in range(-3, 2):
                if n in between:
                    between[n]()
                iteration(Batch(n // 2, n % 2))
            with engine.Fori(1, (B - 2) // 2) as half:
                iteration(Batch(half, 0))
                iteration(Batch(half, 1))
            for n in range(B - 2, B + 1):
                iteration(Batch(n // 2, n % 2))

        def run_stage_two(engine, step, drain):
            def middle(e):
                with engine.Fori(0, NB // 2 - 1) as m:
                    step(e, 2 * m + 1, 1, before=(e, 2 * m))
                    step(e, 2 * m + 2, 0, before=(e, 2 * m + 1))

            step(0, 0, 0, before=None)
            with engine.Fori(0, E - 1) as e:
                middle(e)
                step(e, NB - 1, 1, before=(e, NB - 2), refill_gu=True)
                step(e + 1, 0, 0, before=(e, NB - 1), refill_dn=True)
            middle(E - 1)
            step(E - 1, NB - 1, 1, before=(E - 1, NB - 2))
            drain(E - 1, NB - 1, 1)

        block = ctx.enter_context(nc.Block())

        @block.sync
        def _(sp):
            sp.dma_start(c32, c_t.rearrange("(k p) b -> p k b", p=P)).then_inc(s["c_in"], 16)
            sp.dma_start(wmod32, wmod.rearrange("(k p) n -> p k n", p=P)).then_inc(s["wmod_in"], 16)
            sp.dma_start(bias_p[:, :], bqkv_p).then_inc(s["bias_in"], 16)
            sp.dma_start(wq32, wqkv_t.rearrange("(k p) n -> p k n", p=P)).then_inc(s["wqkv_in"], 16)
            sp.dma_start(wo32, wo_t.rearrange("(k p) n -> p k n", p=P)).then_inc(s["wo_in"], 16)
            sp.dma_start(wr32, router_t.rearrange("(k p) n -> p k n", p=P)).then_inc(s["wo_in"], 16)
            sp.dma_start(bo_bc[:, :], b_o.partition_broadcast(P)).then_inc(s["bo_in"], 16)

            def load_expert(e):
                for g, w in enumerate((gate_t, up_t)):
                    sp.dma_start(staged_gu[:, g * KD:(g + 1) * KD, :],
                                 w[bass.ds(e, 1)].rearrange("a (k p) i -> p (a k) i", p=P)).then_inc(s["gu_in"], 16)
                sp.dma_start(staged_dn.rearrange("p (j d) -> p j d", j=IJ),
                             down_t[bass.ds(e, 1)].rearrange("a (j p) d -> p (a j) d", p=P)).then_inc(s["dn_in"], 16)

            def store_gates():
                wait(sp, s["gates_ready"], 2)
                sp.dma_start(gates_d.rearrange("g b d -> b g d"), gate_r[:, :, :]).then_inc(s["gates_out"], 16)
                wait(sp, s["consts_ready"], 4)
                load_expert(0)

            def iteration(c):
                n, o, ahead = c.at(1), c.at(-1), c.at(2)
                if ahead.real:
                    wait(sp, s["st1_ready"], TT * (ahead.n - 1))
                    sp.dma_start(x1[:, bass.ds(TT * ahead.n, TT), :],
                                 x[bass.ds(ahead.n, 1)].rearrange("a (t p) d -> p (a t) d", p=P)).then_inc(x_in[ahead.par], 16)
                if n.real:
                    wait(sp, stack_in[n.par], 12 * 16 * n.half)
                    wait(sp, s["qh_ready"], n.n + 1)
                    wait(sp, s["ql_ready"], n.n + 1)
                    for part, src in enumerate((qh, ql)):
                        sp.dma_start(q_d[n.par, part].rearrange("(k p) s -> p k s", p=P), src[:, :, :]).then_inc(s["scr_written"], 16)
                if c.real:
                    wait(sp, s["nm_ready"], c.n + 1)
                    for odd in range(2):
                        sp.dma_start(qst[64 * odd + STACK:64 * odd + STACK + 1, c.par, :, :],
                                     nm[PAIRS * odd:PAIRS * (odd + 1), :]).then_inc(nm_in[c.par], 16)
                if n.real:
                    wait(sp, s["kh_ready"], n.n + 1)
                    wait(sp, s["kl_ready"], n.n + 1)
                    for part, src in enumerate((kh, kl)):
                        sp.dma_start(k_d[n.par, part].rearrange("(k p) s -> p k s", p=P), src[:, :, :]).then_inc(s["scr_written"], 16)
                    wait(sp, s["scr_written"], 64 * (n.n + 1))
                    wait(sp, s["scT_done"], PAIRS * n.n - PAIRS)
                    for odd in range(2):
                        for r, (qpart, kpart) in enumerate(((0, 0), (0, 1), (1, 0))):
                            row = 64 * odd + HD * r
                            for stack, scratch, part in ((qst, q_d, qpart), (kst, k_d, kpart)):
                                src = scratch[n.par, part].rearrange("(s o d) t -> o d s t", o=2, d=HD)[odd]
                                sp.dma_start(stack[row:row + HD, n.par, :, :], src).then_inc(stack_in[n.par], 16)
                if c.real:
                    if isinstance(c.n, int) and c.n == 0:
                        wait(sp, s["gates_out"], 16)
                    wait(sp, s["gated_ready"], c.n)
                    sp.dma_start(ga_bc[:, :], gates_d[0, bass.ds(c.n, 1), :].rearrange("a d -> (a d)").partition_broadcast(P)).then_inc(s["ga_in"], 16)

            run_stage_one(sp, iteration, {-1: store_gates})

            with sp.Fori(1, E) as e:
                wait(sp, s["wgu_h"], IJ * e)
                wait(sp, s["wgu_l"], IJ * e)
                wait(sp, s["wdn_h"], e)
                wait(sp, s["wdn_l"], e)
                load_expert(e)
            def finish(blk):
                sp.dma_start(gb_bc[:, :, :].rearrange("p b d -> p (b d)"),
                             gates_d[1, bass.ds(2 * blk, 2), :].rearrange("b d -> (b d)").partition_broadcast(P)).then_inc(s["gb_in"], 16)
                wait(sp, s["fin_add"], blk + 1)
                sp.dma_start(out[bass.ds(2 * blk, 2)].rearrange("b (t p) d -> p (b t) d", p=P),
                             acc[:, bass.ds(BT * blk, BT), :]).then_inc(s["out_done"], 16)

            with sp.Fori(0, NB) as blk:
                finish(blk)
            wait(sp, s["out_done"], 16 * NB)

        @block.gpsimd
        def _(pool):
            pool.memset(ident[:, :], 0.0).then_inc(s["ident_ready"], 1)
            pool.wait_ge(s["ident_ready"], 1)
            pool.affine_select(out=ident[:, :], in_=ident[:, :], compare_op=ALU.not_equal, fill=1.0, base=0,
                               pattern=[[-1, P]], channel_multiplier=1).then_inc(s["ident_ready"], 1)
            pool.memset(halfpow[:, :], -0.5).then_inc(s["pow_ready"], 1)
            pool.memset(eps[:, :], EPS).then_inc(s["pow_ready"], 1)
            pool.wait_ge(s["pow_ready"], 2)
            pool.memset(earlier[:, :, :], 1.0).then_inc(s["consts_ready"], 1)
            pool.wait_ge(s["consts_ready"], 1)
            pool.affine_select(out=earlier[:, :, :], in_=earlier[:, :, :], compare_op=ALU.is_gt, fill=0.0, base=0,
                               pattern=[[1, E], [-1, E]], channel_multiplier=0).then_inc(s["consts_ready"], 1)
            pool.memset(kst[:, :, :, :].rearrange("p a b c -> p (a b c)"), MAXK).then_inc(s["consts_ready"], 1)
            pool.memset(vx[:, :, :, :, :].rearrange("p a b c d -> p (a b c d)"), 1.0).then_inc(s["consts_ready"], 1)

            def clear_acc():
                pool.wait_ge(s["mod_done"], 2)
                pool.wait_ge(s["siluc_ready"], 1)
                pool.wait_ge(s["wsplit_h"], 3)
                pool.wait_ge(s["wsplit_l"], 3)
                for q in range(4):
                    pool.memset(acc[:, q * NT // 4:(q + 1) * NT // 4, :].rearrange("p t d -> p (t d)"), 0.0).then_inc(s["acc_ready"], 1)

            def inverse_deviation(mv, ve, rs, mv_sem, ve_sem, rs_sem, n):
                pool.wait_ge(s[mv_sem], TT * (n + 1))
                pool.tensor_tensor(ve[:, :], mv[:, :, 1], eps[:, :], ALU.add).then_inc(s[ve_sem], 1)
                pool.wait_ge(s[ve_sem], n + 1)
                pool.tensor_tensor(rs[:, :], ve[:, :], halfpow[:, :], ALU.pow).then_inc(s[rs_sem], 1)

            def iteration(c):
                n, o, m = c.at(1), c.at(-1), c.at(2)
                if n.real:
                    wait(pool, s["kh_ready"], n.n + 1)
                    wait(pool, s["scr_written"], 64 * n.n)
                    pool.tensor_tensor(kl[:, :, :], k32[:, :, :], kh[:, :, :], ALU.subtract).then_inc(s["kl_ready"], 1)
                if o.real:
                    wait(pool, s["proj_ready"], o.n + 1)
                    wait(pool, s["ga_in"], 16 * (o.n + 1))
                    pool.tensor_tensor(gated[:, :, :], proj[:, :, :], ga_bc[:, :].unsqueeze(1).to_broadcast([P, TT, D]),
                                       ALU.mult).then_inc(s["gated_ready"], 1)
                    wait(pool, s["gated_ready"], o.n + 1)
                    tile = x1[:, bass.ds(TT * o.n, TT), :]
                    pool.tensor_tensor(tile, tile, gated[:, :, :], ALU.add).then_inc(s["x1_ready"], 1)
                if m.real:
                    inverse_deviation(mv1, ve1, rs1, "mv1_ready", "ve1_ready", "rs1_ready", m.n)
                if o.real:
                    inverse_deviation(mv2, ve2, rs2, "mv2_ready", "ve2_ready", "rs2_ready", o.n)

            run_stage_one(pool, iteration, {0: clear_acc})

            with pool.Fori(0, NB) as blk:
                pool.wait_ge(s["acc_ready"], 4 + BT * (NB * (E - 1) + blk + 1))
                pool.wait_ge(s["gb_in"], 16 * (blk + 1))
                for b in range(2):
                    tiles = acc[:, bass.ds(BT * blk + TT * b, TT), :]
                    pool.tensor_tensor(tiles, tiles, gb_bc[:, b, :].unsqueeze(1).to_broadcast([P, TT, D]),
                                       ALU.mult).then_inc(s["fin_mul"], 1)
                pool.wait_ge(s["fin_mul"], 2 * (blk + 1))
                tiles = acc[:, bass.ds(BT * blk, BT), :]
                pool.tensor_tensor(tiles, tiles, x1[:, bass.ds(BT * blk, BT), :], ALU.add).then_inc(s["fin_add"], 1)

        @block.scalar
        def _(act):
            act.wait_ge(s["c_in"], 16)
            act.activation(tanh_c[:, :, :], c32, ACT.Tanh, scale=0.5).then_inc(s["tanhc_ready"], 1)
            act.wait_ge(s["wqkv_in"], 16)
            act.activation(wq_h[:, :, :], wq32, ACT.Copy, scale=WS).then_inc(s["wsplit_h"], 1)
            act.wait_ge(s["wo_in"], 32)
            act.activation(wo_h[:, :, :], wo32, ACT.Copy, scale=WS).then_inc(s["wsplit_h"], 1)
            act.activation(wr_h[:, :, :], wr32, ACT.Copy, scale=WS).then_inc(s["wsplit_h"], 1)

            def modulated(dst, src, norm, n, done):
                for k in range(KD):
                    act.activation(dst[:, k, :], src[:, k, :], ACT.Identity, scale=modv[:, 2 * norm + 1, k, bass.ds(n, 1)],
                                   bias=modv[:, 2 * norm, k, bass.ds(n, 1)]).then_inc(s[done], 1)

            def iteration(c):
                n, o = c.at(1), c.at(-1)
                misc = [bank[:, 6 + i, :].rearrange("p (k s) -> p k s", k=2) for i in range(2)]
                if n.real:
                    if isinstance(n.n, int) and n.n == 0:
                        act.wait_ge(s["modv_ready"], 2)
                        act.wait_ge(s["bias_s_ready"], 3)
                    wait(act, s["t1_done"], n.n + 1)
                    wait(act, s["hl_ready"], n.n)
                    modulated(hT, misc[0], 0, n.n, "hT_ready")
                    wait(act, s["hT_ready"], 2 * (n.n + 1))
                    wait(act, s["vp_done"], n.n)
                    act.activation(hh[:, :, :], hT[:, :, :], ACT.Copy).then_inc(s["hh_ready"], 1)
                    wait(act, s["qp_done"], n.n + 1)
                    wait(act, s["ql_ready"], n.n)
                    for m in range(2):
                        act.activation(q32[:, m, :], misc[1][:, m, :], ACT.Identity, scale=QS / GU_SCALE,
                                       bias=bias_s[:, m:m + 1]).then_inc(s["q32_ready"], 1)
                    wait(act, s["q32_ready"], 2 * (n.n + 1))
                    wait(act, s["scr_written"], 64 * n.n)
                    act.activation(qh[:, :, :], q32[:, :, :], ACT.Copy).then_inc(s["qh_ready"], 1)
                    wait(act, s["kp_done"], n.n + 1)
                    wait(act, s["kl_ready"], n.n)
                    for m in range(2):
                        act.activation(k32[:, m, :], misc[0][:, m, :], ACT.Identity, scale=XS / GU_SCALE,
                                       bias=bias_s[:, 2 + m:3 + m]).then_inc(s["k32_ready"], 1)
                    wait(act, s["k32_ready"], 2 * (n.n + 1))
                    act.activation(kh[:, :, :], k32[:, :, :], ACT.Copy).then_inc(s["kh_ready"], 1)
                if o.real:
                    wait(act, s["ta_done"], o.n + 1)
                    wait(act, s["al_ready"], o.n)
                    for k in range(KD):
                        act.activation(aT[:, k, :], misc[1][:, k, :], ACT.Identity, scale=XS,
                                       bias=bias_s[:, 4 + k:5 + k]).then_inc(s["aT_ready"], 1)
                    wait(act, s["aT_ready"], 2 * (o.n + 1))
                    wait(act, s["op_done"], o.n)
                    act.activation(ah[:, :, :], aT[:, :, :], ACT.Copy).then_inc(s["ah_ready"], 1)
                if n.real:
                    wait(act, s["vp_done"], n.n + 1)
                    wait(act, s["pv_done"], PAIRS * (n.n - 1))
                    if isinstance(n.n, int) and n.n < 2:
                        act.wait_ge(s["consts_ready"], 4)
                    for t in range(TT):
                        act.activation(vx[:, n.par, t, :, 0:HD], misc[0][:, t, :].rearrange("p (h d) -> p h d", h=H),
                                       ACT.Copy, scale=1.0 / GU_SCALE).then_inc(s["v_ready"], 1)
                for pair in range(PAIRS):
                    if c.real:
                        wait(act, s["scT_done"], PAIRS * c.n + pair + 1)
                        wait(act, s["pv_done"], PAIRS * c.n + pair - 1)
                        r = 2 * (pair % 2)
                        act.activation(prob[:, pair % 2, :, :, :].rearrange("p a b c -> p (a b c)"),
                                       bank[:, r:r + 2, :].rearrange("p a b -> p (a b)"),
                                       ACT.Exp, scale=1.0 / SS).then_inc(s["exp_done"], 1)
                        if pair in (5, 7):
                            half = (pair - 5) // 2
                            wait(act, s["pv_done"], PAIRS * c.n + 4 * (half + 1))
                            wait(act, s["tn_done"], TT * c.n)
                            act.activation(au[:, 2 * half:2 * half + 2, :].rearrange("p g s -> p (g s)"), bank[:, 4 + half, :],
                                           ACT.Copy).then_inc(s["au_ready"], 1)
                    if o.real and pair == 5:
                        wait(act, s["t2_done"], o.n + 1)
                        wait(act, s["h2l_ready"], o.n)
                        modulated(h2T, misc[1], 1, o.n, "h2T_ready")
                        wait(act, s["h2T_ready"], 2 * (o.n + 1))
                        act.activation(h2h[:, :, bass.ds(S * o.n, S)], h2T[:, :, :], ACT.Copy).then_inc(s["h2h_ready"], 1)
                if o.real:
                    wait(act, s["lsh_ready"], o.n + 1)
                    wait(act, s["w_ready"], o.n)
                    act.activation(pexp[:, :, :], lsh[:, :, :], ACT.Exp, scale=1.0 / GU_SCALE).then_inc(s["pexp_ready"], 1)

            run_stage_one(act, iteration)

            def split_gu(e, j):
                act.activation(gu_h[:, j, :].rearrange("p (g m) -> p g m", g=2 * KD), staged_gu[:, :, j * P:(j + 1) * P],
                               ACT.Copy, scale=WS).then_inc(s["wgu_h"], 1)

            def split_dn(e):
                act.wait_ge(s["dn_in"], 16 * (e + 1))
                act.activation(dn_h[:, :, :].rearrange("p j d -> p (j d)"), staged_dn, ACT.Copy, scale=WS).then_inc(s["wdn_h"], 1)

            def step(e, blk, par, before, refill_gu=False, refill_dn=False):
                done = IJ * (NB * e + blk)
                for j in range(IJ):
                    wait(act, s["gu_done"], done + j + 1)
                    wait(act, s["sg_ready"], done + j - 1)
                    act.activation(th[j % 2], bank[:, 2 * (j % 2), :], ACT.Tanh, scale=0.5 / GU_SCALE).then_inc(s["th_ready"], 1)
                    wait(act, s["hf_ready"], done + j + 1)
                    act.activation(hid_h[:, par, j, :], hf[j % 2], ACT.Copy).then_inc(s["hidh_ready"], 1)
                    if refill_gu:
                        if j == 0:
                            act.wait_ge(s["gu_in"], 32 * (e + 2))
                        split_gu(e + 1, j)
                if refill_dn:
                    wait(act, s["y_done"], BT * NB * e)
                    split_dn(e)

            act.wait_ge(s["gu_in"], 32)
            for j in range(IJ):
                split_gu(0, j)
            split_dn(0)
            run_stage_two(act, step, lambda e, blk, par: None)

        @block.vector
        def _(dve):
            dve.wait_ge(s["tanhc_ready"], 1)
            dve.scalar_tensor_tensor(out=silu_c[:, :, :], in0=tanh_c[:, :, :], scalar=1.0, in1=c32,
                                     op0=ALU.add, op1=ALU.mult).then_inc(s["siluc_ready"], 1)
            dve.wait_ge(s["bias_in"], 16)
            for first, scale in ((0, QS), (2, XS), (4, XS)):
                dve.tensor_scalar(bias_s[:, first:first + 2], bias_p[:, first:first + 2], scale, None,
                                  ALU.mult).then_inc(s["bias_s_ready"], 1)
            dve.wait_ge(s["mod_done"], 1)
            made = bank[:, 6, 0:4 * KD * B].rearrange("p (l w n) -> p l w n", l=2, w=2)
            kept = modv[:, :, :, :].rearrange("p (l w) k b -> p l w (k b)", w=2)
            dve.tensor_scalar(kept[:, :, 0, :], made[:, :, 0, :], XS / 2, None, ALU.mult).then_inc(s["modv_ready"], 1)
            dve.tensor_scalar(kept[:, :, 1, :], made[:, :, 1, :], XS / 2, XS, ALU.mult, ALU.add).then_inc(s["modv_ready"], 1)
            dve.wait_ge(s["mod_done"], 2)
            rows = bank[0:B, 7, :].rearrange("b (g d) -> b g d", g=2)
            dve.tensor_scalar(gate_r[:, :, :], rows, 0.5, None, ALU.mult).then_inc(s["gr_ready"], 1)
            dve.wait_ge(s["gr_ready"], 1)
            dve.tensor_scalar(gate_s[:, :, :], gate_r[:, :, :], 0.0, 2.0, ALU.is_ge, ALU.mult).then_inc(s["gr_ready"], 1)
            dve.wait_ge(s["gr_ready"], 2)
            dve.scalar_tensor_tensor(out=gate_m[:, :, :], in0=gate_s[:, :, :], scalar=-1.0, in1=gate_r[:, :, :],
                                     op0=ALU.add, op1=ALU.mult).then_inc(s["gr_ready"], 1)
            dve.wait_ge(s["gr_ready"], 3)
            for g, scale in enumerate((1.0, 1.0 / WS)):
                dve.tensor_scalar(gate_m[:, g, :], gate_m[:, g, :], GATE_MIN, scale, ALU.max, ALU.mult).then_inc(s["gr_ready"], 1)
            dve.wait_ge(s["gr_ready"], 5)
            for g in range(2):
                dve.scalar_tensor_tensor(out=gate_r[:, g, :], in0=gate_s[:, g, :], scalar=-1.0, in1=gate_m[:, g, :],
                                         op0=ALU.add, op1=ALU.mult).then_inc(s["gates_ready"], 1)
            for count, (lo, full, hi) in enumerate(((wq_l, wq32, wq_h), (wo_l, wo32, wo_h), (wr_l, wr32, wr_h))):
                dve.wait_ge(s["wsplit_h"], count + 1)
                dve.scalar_tensor_tensor(out=lo[:, :, :], in0=full, scalar=WS, in1=hi[:, :, :],
                                         op0=ALU.mult, op1=ALU.subtract).then_inc(s["wsplit_l"], 1)
            dve.wait_ge(s["consts_ready"], 2)
            dve.wait_ge(s["bo_in"], 16)

            def statistics(stats, parts, mv, of, n):
                stats_sem, halves_sem, parts_sem, mv_sem = (s[f"{name}{of}_ready"] for name in ("st", "halves", "parts", "mv"))
                for t in range(TT):
                    dve.bn_stats(stats[:, t, :], x1[:, bass.ds(TT * n + t, 1), :].rearrange("p a d -> p (a d)")).then_inc(stats_sem, 1)
                wait(dve, stats_sem, TT * (n + 1))
                even, odd = stats[:, :, 1:3], stats[:, :, 4:6]
                total, apart, apart2 = parts[:, :, 0:2], parts[:, :, 2], parts[:, :, 3]
                dve.tensor_tensor(total, even, odd, ALU.add).then_inc(halves_sem, 1)
                dve.tensor_tensor(apart, even[:, :, 0], odd[:, :, 0], ALU.subtract).then_inc(halves_sem, 1)
                wait(dve, halves_sem, 2 * (n + 1))
                dve.scalar_tensor_tensor(out=apart2, in0=apart, scalar=0.25, in1=apart, op0=ALU.mult, op1=ALU.mult).then_inc(parts_sem, 1)
                dve.tensor_scalar(mv[:, :, 0], total[:, :, 0], 0.5, None, ALU.mult).then_inc(mv_sem, 1)
                wait(dve, parts_sem, n + 1)
                dve.scalar_tensor_tensor(out=mv[:, :, 1], in0=total[:, :, 1], scalar=1.0 / D, in1=apart2,
                                         op0=ALU.mult, op1=ALU.add).then_inc(mv_sem, 1)

            def normalise(xn, mv, rs, done, n):
                for t in range(TT):
                    dve.tensor_scalar(xn[:, t, :], x1[:, bass.ds(TT * n + t, 1), :].rearrange("p a d -> p (a d)"),
                                      mv[:, t, 0:1], rs[:, t:t + 1], ALU.subtract, ALU.mult).then_inc(s[done], 1)

            def route(o):
                wait(dve, s["rt_done"], o + 1)
                logits = bank[:, 6, 0:TT * E].rearrange("p (t e) -> p t e", t=TT)
                dve.tensor_reduce(lmax[:, :], logits, AX.X, ALU.max).then_inc(s["lmax_ready"], 1)
                wait(dve, s["lmax_ready"], o + 1)
                dve.tensor_tensor(lsh[:, :, :], logits, lmax[:, :].unsqueeze(2).to_broadcast([P, TT, E]),
                                  ALU.subtract).then_inc(s["lsh_ready"], 1)
                wait(dve, s["pexp_ready"], o + 1)
                dve.tensor_reduce(psum_r[:, :], pexp[:, :, :], AX.X, ALU.add).then_inc(s["rsum_ready"], 1)
                wait(dve, s["rsum_ready"], o + 1)
                dve.reciprocal(prec[:, :], psum_r[:, :]).then_inc(s["prec_ready"], 1)
                wait(dve, s["prec_ready"], o + 1)
                dve.tensor_tensor(rp[:, :, :], pexp[:, :, :], prec[:, :].unsqueeze(2).to_broadcast([P, TT, E]),
                                  ALU.mult).then_inc(s["rp_ready"], 1)
                wait(dve, s["rp_ready"], o + 1)
                mine = rp[:, :, :].unsqueeze(3).to_broadcast([P, TT, E, E])
                other = rp[:, :, :].unsqueeze(2).to_broadcast([P, TT, E, E])
                dve.tensor_tensor(before[:, :, :, :], other, mine, ALU.is_gt).then_inc(s["before_ready"], 1)
                dve.tensor_tensor(ties[:, :, :, :], other, mine, ALU.is_equal).then_inc(s["ties_ready"], 1)
                wait(dve, s["ties_ready"], o + 1)
                dve.tensor_tensor(ties[:, :, :, :], ties[:, :, :, :], earlier[:, :, :].unsqueeze(1).to_broadcast([P, TT, E, E]),
                                  ALU.mult).then_inc(s["tied_ready"], 1)
                wait(dve, s["tied_ready"], o + 1)
                dve.tensor_tensor(before[:, :, :, :], before[:, :, :, :], ties[:, :, :, :], ALU.add).then_inc(s["joined_ready"], 1)
                wait(dve, s["joined_ready"], o + 1)
                dve.tensor_tensor(ties[:, :, :, :], before[:, :, :, :], other, ALU.mult).then_inc(s["weighed_ready"], 1)
                wait(dve, s["weighed_ready"], o + 1)
                dve.tensor_reduce(cum[:, :, :], ties[:, :, :, :], AX.X, ALU.add).then_inc(s["cum_ready"], 1)
                wait(dve, s["cum_ready"], o + 1)
                dve.scalar_tensor_tensor(out=wts[:, bass.ds(TT * o, TT), :], in0=cum[:, :, :], scalar=TOP_P, in1=rp[:, :, :],
                                         op0=ALU.is_le, op1=ALU.mult).then_inc(s["w_ready"], 1)

            def iteration(c):
                n, o, m = c.at(1), c.at(-1), c.at(2)

                def maxima(pair):
                    if not c.real:
                        return
                    wait(dve, s["sc_done"], PAIRS * c.n + pair + 1)
                    if pair == 0:
                        wait(dve, s["nmt_done"], c.n)
                    r = 2 * (pair % 2)
                    dve.tensor_reduce(mx[:, :, :, pair].rearrange("p t o -> p o t"),
                                      bank[:, r:r + 2, :].rearrange("p o (t s) -> p o t s", t=TT),
                                      AX.X, ALU.max).then_inc(s["max_done"], 1)

                maxima(0)
                maxima(1)
                maxima(2)
                if o.real:
                    wait(dve, s["ta_done"], o.n)
                    for t in range(TT):
                        heads = bank[:, 7 - t, :].rearrange("p (h w) -> p h w", h=H)
                        wait(dve, s["tn_done"], TT * o.n + t + 1)
                        dve.reciprocal(rec[:, t, :], heads[:, :, HD]).then_inc(s["rec_ready"], 1)
                        wait(dve, s["rec_ready"], TT * o.n + t + 1)
                        dve.tensor_tensor(at[:, t, :].rearrange("p (h d) -> p h d", h=H), heads[:, :, 0:HD],
                                          rec[:, t, :].unsqueeze(2).to_broadcast([P, H, HD]), ALU.mult).then_inc(s["at_ready"], 1)
                maxima(3)
                if n.real:
                    wait(dve, s["hh_ready"], n.n + 1)
                    wait(dve, s["vp_done"], n.n)
                    dve.tensor_tensor(hl[:, :, :], hT[:, :, :], hh[:, :, :], ALU.subtract).then_inc(s["hl_ready"], 1)
                maxima(4)
                maxima(5)
                if n.real:
                    wait(dve, s["qh_ready"], n.n + 1)
                    dve.tensor_tensor(ql[:, :, :], q32[:, :, :], qh[:, :, :], ALU.subtract).then_inc(s["ql_ready"], 1)
                maxima(6)
                if o.real:
                    wait(dve, s["ah_ready"], o.n + 1)
                    dve.tensor_tensor(al[:, :, :], aT[:, :, :], ah[:, :, :], ALU.subtract).then_inc(s["al_ready"], 1)
                maxima(7)
                if c.real:
                    wait(dve, s["nmt_done"], c.n + 1)
                    wait(dve, nm_in[1 - c.par], 32 * (c.at(-1).half + 1))
                    dve.tensor_scalar(nm[:, :], bank[0:H, 7, 0:S], -1.0 / MAXK, None, ALU.mult).then_inc(s["nm_ready"], 1)
                if o.real:
                    wait(dve, s["op_done"], o.n + 1)
                    wait(dve, s["gated_ready"], o.n)
                    dve.scalar_tensor_tensor(out=proj[:, :, :], in0=bank[:, 6, :].rearrange("p (t d) -> p t d", t=TT),
                                             scalar=1.0 / GU_SCALE, in1=bo_bc[:, :].unsqueeze(1).to_broadcast([P, TT, D]),
                                             op0=ALU.mult, op1=ALU.add).then_inc(s["proj_ready"], 1)
                if m.real:
                    wait(dve, x_in[m.par], 16 * (m.half + 1))
                    statistics(bn1, parts1, mv1, 1, m.n)
                if o.real:
                    wait(dve, s["x1_ready"], o.n + 1)
                    statistics(bn2, parts2, mv2, 2, o.n)
                if m.real:
                    wait(dve, s["rs1_ready"], m.n + 1)
                    wait(dve, s["t1_done"], m.n)
                    normalise(xn1, mv1, rs1, "xn1_ready", m.n)
                if o.real:
                    wait(dve, s["rs2_ready"], o.n + 1)
                    normalise(xn2, mv2, rs2, "xn2_ready", o.n)
                    wait(dve, s["h2h_ready"], o.n + 1)
                    dve.tensor_tensor(h2l[:, :, bass.ds(S * o.n, S)], h2T[:, :, :], h2h[:, :, bass.ds(S * o.n, S)],
                                      ALU.subtract).then_inc(s["h2l_ready"], 1)
                    route(o.n)

            run_stage_one(dve, iteration)

            def split_gu(count, j):
                dve.wait_ge(s["wgu_h"], count)
                dve.scalar_tensor_tensor(out=gu_l[:, j, :].rearrange("p (g m) -> p g m", g=2 * KD),
                                         in0=staged_gu[:, :, j * P:(j + 1) * P], scalar=WS,
                                         in1=gu_h[:, j, :].rearrange("p (g m) -> p g m", g=2 * KD),
                                         op0=ALU.mult, op1=ALU.subtract).then_inc(s["wgu_l"], 1)

            def split_dn(e):
                dve.wait_ge(s["wdn_h"], e + 1)
                dve.scalar_tensor_tensor(out=dn_l[:, :, :].rearrange("p j d -> p (j d)"), in0=staged_dn, scalar=WS,
                                         in1=dn_h[:, :, :].rearrange("p j d -> p (j d)"),
                                         op0=ALU.mult, op1=ALU.subtract).then_inc(s["wdn_l"], 1)

            def add_share(e, blk, t):
                done = BT * (NB * e + blk) + t
                wait(dve, s["y_done"], done + 1)
                if isinstance(done, int) and done == 0:
                    wait(dve, s["acc_ready"], 4)
                tile = acc[:, bass.ds(BT * blk + t, 1), :].rearrange("p a d -> p (a d)")
                dve.scalar_tensor_tensor(out=tile, in0=bank[:, 4 + t, 0:D],
                                         scalar=wts[:, bass.ds(BT * blk + t, 1), bass.ds(e, 1)].rearrange("p a b -> p (a b)"),
                                         in1=tile, op0=ALU.mult, op1=ALU.add).then_inc(s["acc_ready"], 1)

            def step(e, blk, par, before, refill_gu=False, refill_dn=False):
                done = IJ * (NB * e + blk)
                for j in range(IJ):
                    wait(dve, s["th_ready"], done + j + 1)
                    dve.scalar_tensor_tensor(out=sg[j % 2], in0=th[j % 2], scalar=1.0, in1=bank[:, 2 * (j % 2), :],
                                             op0=ALU.add, op1=ALU.mult).then_inc(s["sg_ready"], 1)
                    wait(dve, s["sg_ready"], done + j + 1)
                    dve.scalar_tensor_tensor(out=hf[j % 2], in0=sg[j % 2], scalar=0.5 / GU_SCALE ** 2,
                                             in1=bank[:, 2 * (j % 2) + 1, :], op0=ALU.mult, op1=ALU.mult).then_inc(s["hf_ready"], 1)
                    if before is not None:
                        add_share(*before, j)
                    wait(dve, s["hidh_ready"], done + j + 1)
                    dve.tensor_tensor(hid_l[:, par, j, :], hf[j % 2], hid_h[:, par, j, :], ALU.subtract).then_inc(s["hidl_ready"], 1)
                    if refill_gu:
                        split_gu(IJ * (e + 1) + j + 1, j)
                if refill_dn:
                    split_dn(e)

            def drain(e, blk, par):
                for t in range(BT):
                    add_share(e, blk, t)

            for j in range(IJ):
                split_gu(j + 1, j)
            split_dn(0)
            run_stage_two(dve, step, drain)

        @block.tensor
        def _(pe):
            pe.wait_ge(s["siluc_ready"], 1)
            pe.wait_ge(s["wmod_in"], 16)
            for q, col in enumerate((0, 1, 3, 4)):
                for m in range(KD):
                    at_col = (q * KD + m) * B
                    for k in range(KD):
                        mm = pe.matmul(bank[:, 6, at_col:at_col + B], wmod32[:, k, col * D + m * P:col * D + (m + 1) * P],
                                       silu_c[:, k, :], start=(k == 0), stop=(k == KD - 1))
            mm.then_inc(s["mod_done"], 1)
            for g, col in enumerate((2, 5)):
                for k in range(KD):
                    mm = pe.matmul(bank[0:B, 7, g * D:(g + 1) * D], silu_c[:, k, :], wmod32[:, k, col * D:(col + 1) * D],
                                   start=(k == 0), stop=(k == KD - 1))
            mm.then_inc(s["mod_done"], 1)
            pe.wait_ge(s["ident_ready"], 2)
            pe.wait_ge(s["wsplit_l"], 3)
            pe.wait_ge(s["modv_ready"], 2)
            pe.wait_ge(s["gr_ready"], 1)

            def product(dst, weights, moving, pieces, count=None):
                terms = [pair for k in range(pieces) for pair in passes(*weights(k), *moving(k))]
                for i, (w, a) in enumerate(terms):
                    mm = pe.matmul(dst, w, a, start=(i == 0), stop=(i == len(terms) - 1))
                return mm

            def iteration(c):
                n, o = c.at(1), c.at(-1)

                def scores(pair):
                    if not c.real:
                        return
                    if pair == 0:
                        wait(pe, stack_in[c.par], 12 * 16 * (c.half + 1))
                    if pair < 2:
                        wait(pe, s["exp_done"], PAIRS * c.n - 1 + pair)
                    else:
                        wait(pe, s["max_done"], PAIRS * c.n + pair - 1)
                    for t in range(TT):
                        for odd in range(2):
                            rows = slice(64 * odd, 64 * odd + STACK)
                            mm = pe.matmul(bank[:, 2 * (pair % 2) + odd, t * S:(t + 1) * S],
                                           qst[rows, c.par, pair, t * P:(t + 1) * P], kst[rows, c.par, pair, :],
                                           start=True, stop=True)
                    mm.then_inc(s["sc_done"], 1)

                def scores_transposed(pair):
                    if not c.real:
                        return
                    if pair == 0:
                        wait(pe, nm_in[c.par], 32 * (c.half + 1))
                    if pair < 2:
                        wait(pe, s["max_done"], PAIRS * c.n + PAIRS - 1 + pair)
                    else:
                        wait(pe, s["exp_done"], PAIRS * c.n + pair - 1)
                    for t in range(TT):
                        for odd in range(2):
                            rows = slice(64 * odd, 64 * odd + STACK + 1)
                            mm = pe.matmul(bank[:, 2 * (pair % 2) + odd, t * S:(t + 1) * S],
                                           kst[rows, c.par, pair, t * P:(t + 1) * P], qst[rows, c.par, pair, :],
                                           start=True, stop=True)
                    mm.then_inc(s["scT_done"], 1)

                def weighted_values(pair):
                    if not c.real:
                        return
                    group = pair // 2
                    wait(pe, s["exp_done"], PAIRS * c.n + pair + 1)
                    if pair == 0:
                        wait(pe, s["v_ready"], TT * (c.n + 1))
                    if pair % 4 == 0:
                        wait(pe, s["au_ready"], 2 * c.n - 1 + pair // 4)
                    for t in range(TT):
                        for odd in range(2):
                            col = 2 * (pair % 2) + odd
                            mm = pe.matmul(bank[VW * col:VW * (col + 1), 4 + group // 2, (group % 2) * S:(group % 2 + 1) * S],
                                           vx[:, c.par, t, 2 * pair + odd, :], prob[:, pair % 2, odd, t, :],
                                           start=(t == 0), stop=(t == TT - 1), skip_group_check=True,
                                           tile_position=(0, VW * col))
                    mm.then_inc(s["pv_done"], 1)

                def transpose_tiles(which, src, done):
                    for k in range(KD):
                        for t in range(TT):
                            mm = pe.transpose(bank[:, which, k * S + t * P:k * S + (t + 1) * P], src[:, t, k * P:(k + 1) * P], ident[:, :])
                    mm.then_inc(s[done], 1)

                def ln1_transposed():
                    if n.real:
                        if isinstance(c.n, int) and c.n < 2:
                            wait(pe, s["v_ready"], TT * n.n)
                        wait(pe, s["w_ready"], c.n - 1)
                        wait(pe, s["xn1_ready"], TT * (n.n + 1))
                        transpose_tiles(6, xn1, "t1_done")

                def attention_by_token():
                    if o.real:
                        wait(pe, s["au_ready"], 2 * (o.n + 1))
                        for t in range(TT):
                            if t == 0:
                                wait(pe, s["h2T_ready"], 2 * o.n)
                            elif n.real:
                                wait(pe, s["hT_ready"], 2 * (n.n + 1))
                            else:
                                wait(pe, s["w_ready"], o.n)
                            for g in range(4):
                                mm = pe.transpose(bank[:, 7 - t, g * P:(g + 1) * P], au[:, g, t * P:(t + 1) * P], ident[:, :])
                            mm.then_inc(s["tn_done"], 1)

                def q_and_k():
                    if n.real:
                        wait(pe, s["hh_ready"], n.n + 1)
                        wait(pe, s["hl_ready"], n.n + 1)
                        for which, (done, piece) in enumerate((("qp_done", 0), ("kp_done", 2))):
                            if o.real:
                                wait(pe, s["at_ready"], TT * o.n + which + 1)
                            elif which == 0:
                                wait(pe, s["q32_ready"], 2 * n.n)
                            else:
                                wait(pe, s["hT_ready"], 2 * (n.n + 1))
                            for m in range(2):
                                cols = slice((piece + m) * P, (piece + m + 1) * P)
                                mm = product(bank[:, 7 - which, m * S:(m + 1) * S],
                                             lambda k: (wq_h[:, k, cols], wq_l[:, k, cols]),
                                             lambda k: (hh[:, k, :], hl[:, k, :]), KD)
                            mm.then_inc(s[done], 1)

                def attention_transposed():
                    if o.real:
                        wait(pe, s["at_ready"], TT * (o.n + 1))
                        if n.real:
                            wait(pe, s["q32_ready"], 2 * (n.n + 1))
                        transpose_tiles(7, at, "ta_done")

                def v():
                    if n.real:
                        wait(pe, s["k32_ready"], 2 * (n.n + 1))
                        for t in range(TT):
                            mm = product(bank[:, 6, t * D:(t + 1) * D],
                                         lambda k: (hh[:, k, t * P:(t + 1) * P], hl[:, k, t * P:(t + 1) * P]),
                                         lambda k: (wq_h[:, k, 2 * D:3 * D], wq_l[:, k, 2 * D:3 * D]), KD)
                        mm.then_inc(s["vp_done"], 1)

                def maxima_transposed():
                    if c.real:
                        wait(pe, s["max_done"], PAIRS * (c.n + 1))
                        if o.real:
                            wait(pe, s["aT_ready"], 2 * (o.n + 1))
                        elif n.real:
                            wait(pe, s["q32_ready"], 2 * (n.n + 1))
                        for t in range(TT):
                            mm = pe.transpose(bank[0:H, 7, t * P:(t + 1) * P],
                                              mx[:, t, :, :].rearrange("p o s -> p (o s)"), ident[:, :])
                        mm.then_inc(s["nmt_done"], 1)

                def output_projection():
                    if o.real:
                        wait(pe, s["ah_ready"], o.n + 1)
                        wait(pe, s["al_ready"], o.n + 1)
                        if n.real:
                            wait(pe, s["v_ready"], TT * (n.n + 1))
                        for t in range(TT):
                            mm = product(bank[:, 6, t * D:(t + 1) * D],
                                         lambda k: (ah[:, k, t * P:(t + 1) * P], al[:, k, t * P:(t + 1) * P]),
                                         lambda k: (wo_h[:, k, :], wo_l[:, k, :]), KD)
                        mm.then_inc(s["op_done"], 1)

                def ln2_transposed():
                    if o.real:
                        wait(pe, s["xn2_ready"], TT * (o.n + 1))
                        if c.real:
                            wait(pe, s["nm_ready"], c.n + 1)
                        transpose_tiles(7, xn2, "t2_done")

                def router():
                    if o.real:
                        wait(pe, s["h2h_ready"], o.n + 1)
                        wait(pe, s["h2l_ready"], o.n + 1)
                        for t in range(TT):
                            tokens = bass.ds(S * o.n + t * P, P)
                            mm = product(bank[:, 6, t * E:(t + 1) * E],
                                         lambda k: (h2h[:, k, tokens], h2l[:, k, tokens]),
                                         lambda k: (wr_h[:, k, :], wr_l[:, k, :]), KD)
                        mm.then_inc(s["rt_done"], 1)

                scores(0)
                scores(1)
                ln1_transposed()
                scores(2)
                attention_by_token()
                scores(3)
                scores(4)
                q_and_k()
                scores(5)
                attention_transposed()
                scores(6)
                v()
                scores(7)
                maxima_transposed()
                output_projection()
                scores_transposed(0)
                scores_transposed(1)
                for pair in range(PAIRS):
                    weighted_values(pair)
                    if pair + 2 < PAIRS:
                        scores_transposed(pair + 2)
                    if pair == 3:
                        ln2_transposed()
                    if pair == 6:
                        router()

            run_stage_one(pe, iteration)

            def gate_up(e, blk, j, first):
                done = IJ * (NB * e + blk)
                if first:
                    wait(pe, s["wgu_l"], IJ * e + j + 1)
                wait(pe, s["hf_ready"], done + j - 1)
                tokens = bass.ds(TB * blk, TB)
                for g in range(2):
                    mm = product(bank[:, 2 * (j % 2) + g, :],
                                 lambda k: (gu_h[:, j, (g * KD + k) * P:(g * KD + k + 1) * P],
                                            gu_l[:, j, (g * KD + k) * P:(g * KD + k + 1) * P]),
                                 lambda k: (h2h[:, k, tokens], h2l[:, k, tokens]), KD)
                mm.then_inc(s["gu_done"], 1)

            def down(e, blk, par, t):
                done = BT * (NB * e + blk)
                if t == 0:
                    wait(pe, s["wdn_l"], e + 1)
                    wait(pe, s["hidl_ready"], IJ * (NB * e + blk + 1))
                wait(pe, s["acc_ready"], done + t + 1)
                mm = product(bank[:, 4 + t, 0:D],
                             lambda j: (hid_h[:, par, j, t * P:(t + 1) * P], hid_l[:, par, j, t * P:(t + 1) * P]),
                             lambda j: (dn_h[:, j, :], dn_l[:, j, :]), IJ)
                mm.then_inc(s["y_done"], 1)

            def step(e, blk, par, before, refill_gu=False, refill_dn=False):
                for j in range(IJ):
                    gate_up(e, blk, j, first=(before is None or refill_dn))
                    if before is not None:
                        down(*before, 1 - par, j)

            def drain(e, blk, par):
                for t in range(BT):
                    down(e, blk, par, t)

            pe.wait_ge(s["w_ready"], B)
            run_stage_two(pe, step, drain)


def kernel(**inputs):
    import numpy as np
    import concourse.bacc as bacc
    from concourse.bass_utils import run_bass_kernel_spmd

    t = lambda name: np.asarray(inputs[name])
    arrays = {
        "x": t("L0_attn_x"),
        "wqkv_t": t("L0_attn_w_qkv").T,
        "bqkv_p": t("L0_attn_b_qkv").reshape(6, P).T,
        "wo_t": t("L0_attn_w_o").T,
        "b_o": t("L0_attn_b_o"),
        "router_t": t("L0_ffn_router_w").T,
        "gate_t": t("L0_ffn_gate_w").transpose(0, 2, 1),
        "up_t": t("L0_ffn_up_w").transpose(0, 2, 1),
        "down_t": t("L0_ffn_down_w").transpose(0, 2, 1),
        "c_t": t("L0_c").T,
        "wmod": t("L0_wmod"),
    }
    arrays = {f"in_{k}": np.ascontiguousarray(v) for k, v in arrays.items()}
    nc = bacc.Bacc("TRN2", target_bir_lowering=False, num_devices=1)
    args = [nc.dram_tensor(k, v.shape, mybir.dt.from_np(v.dtype), kind="ExternalInput").ap() for k, v in arrays.items()]
    out = nc.dram_tensor("out", (B, S, D), F32, kind="ExternalOutput").ap()
    adaln_block(nc, *args, out)
    r = run_bass_kernel_spmd(nc, [arrays], core_ids=[0])
    return r.results[0]["out"]
```

```python
from contextlib import ExitStack

import concourse.bass as bass
from concourse import mybir

F32 = mybir.dt.float32
F16 = mybir.dt.float16
ALU = mybir.AluOpType
ACT = mybir.ActivationFunctionType
AX = mybir.AxisListType

P = 128
B, S, D = 16, 256, 256
H, HD = 16, 16
E, I = 8, 512
KD = D // P
TT = S // P
NT = B * TT
PAIRS = H // 2
EPS = 1e-5
TOP_P = 0.9
GATE_MIN = 0.25

XS = 16.0
WS = 256.0
QS = XS / HD ** 0.5
SS = XS * XS
MAXK = 256.0
VW = 32
STACK = 3 * HD

EARLY = 2
LATE = E - EARLY
TB = 512
NB = B * S // TB
BT = TB // P
IJ = I // P
CHUNKS = EARLY * IJ
CLEARED = 4
GU_SCALE = XS * WS
WPIECE = 2 * KD * P
STAGED = 2 * KD * I + IJ * D


class Batch:

    def __init__(self, half, par):
        self.half, self.par = half, par
        self.n = 2 * half + par

    def at(self, d):
        p = self.par + d
        return Batch(self.half + p // 2, p % 2)

    @property
    def real(self):
        return not isinstance(self.n, int) or 0 <= self.n < B


def wait(engine, sem, value):
    if isinstance(value, int) and value <= 0:
        return
    engine.wait_ge(sem, value)


def adaln_block(nc, x, wqkv_t, bqkv_p, wo_t, b_o, router_t, gate_t, up_t, down_t, c_t, wmod, out):
    with ExitStack() as ctx:
        def sb(name, shape, dt=F32):
            return ctx.enter_context(nc.sbuf_tensor(name, shape, dt))

        def sem(name):
            return ctx.enter_context(nc.semaphore(name))

        bank = ctx.enter_context(nc.psum_tensor("bank", [P, 8, 512], F32))

        acc = sb("acc", [P, NT, D])
        h2h = sb("h2h", [P, KD, B * S], F16)
        h2l = sb("h2l", [P, KD, B * S], F16)
        wts = sb("wts", [P, NT, E])
        ident = sb("ident", [P, P])

        wq_h = sb("wq_h", [P, KD, 3 * D], F16)
        wq_l = sb("wq_l", [P, KD, 3 * D], F16)
        wo_h = sb("wo_h", [P, KD, D], F16)
        wo_l = sb("wo_l", [P, KD, D], F16)
        wr_h = sb("wr_h", [P, KD, E], F16)
        wr_l = sb("wr_l", [P, KD, E], F16)
        bias_p = sb("bias_p", [P, 6])
        bias_s = sb("bias_s", [P, 6])
        bo_bc = sb("bo_bc", [P, D])
        silu_c = sb("silu_c", [P, KD, B])
        tanh_c = sb("tanh_c", [P, KD, B])
        modv = sb("modv", [P, 4, KD, B])
        gate_r = sb("gate_r", [B, 2, D])
        gate_s = sb("gate_s", [B, 2, D])
        gate_m = sb("gate_m", [B, 2, D])
        earlier = sb("earlier", [P, E, E])
        halfpow = sb("halfpow", [P, TT])
        eps = sb("eps", [P, TT])

        xa = sb("xa", [P, 2, TT, D])
        xr = sb("xr", [P, 2, TT, D])
        qst = sb("qst", [P, 2, PAIRS, S], F16)
        kst = sb("kst", [P, 2, PAIRS, S], F16)
        vx = sb("vx", [P, 2, TT, H, VW])
        prob = sb("prob", [P, 2, 2, TT, S])
        bn1 = sb("bn1", [P, TT, 6])
        parts1 = sb("parts1", [P, TT, 4])
        mv1 = sb("mv1", [P, TT, 2])
        ve1 = sb("ve1", [P, TT])
        rs1 = sb("rs1", [P, TT])
        xn1 = sb("xn1", [P, TT, D])
        bn2 = sb("bn2", [P, TT, 6])
        parts2 = sb("parts2", [P, TT, 4])
        mv2 = sb("mv2", [P, TT, 2])
        ve2 = sb("ve2", [P, TT])
        rs2 = sb("rs2", [P, TT])
        xn2 = sb("xn2", [P, TT, D])
        hT = sb("hT", [P, KD, S])
        hh = sb("hh", [P, KD, S], F16)
        hl = sb("hl", [P, KD, S], F16)
        q32 = sb("q32", [P, KD, S])
        qh = sb("qh", [P, KD, S], F16)
        ql = sb("ql", [P, KD, S], F16)
        k32 = sb("k32", [P, KD, S])
        kh = sb("kh", [P, KD, S], F16)
        kl = sb("kl", [P, KD, S], F16)
        mx = sb("mx", [P, TT, 2, PAIRS])
        nm = sb("nm", [H, S], F16)
        au = sb("au", [P, 4, S])
        rec = sb("rec", [P, TT, H])
        at = sb("at", [P, TT, D])
        aT = sb("aT", [P, KD, S])
        ah = sb("ah", [P, KD, S], F16)
        al = sb("al", [P, KD, S], F16)
        ga_bc = sb("ga_bc", [P, D])
        proj = sb("proj", [P, TT, D])
        gated = sb("gated", [P, TT, D])
        h2T = sb("h2T", [P, KD, S])
        lmax = sb("lmax", [P, TT])
        lsh = sb("lsh", [P, TT, E])
        pexp = sb("pexp", [P, TT, E])
        psum_r = sb("psum_r", [P, TT])
        prec = sb("prec", [P, TT])
        rp = sb("rp", [P, TT, E])
        before = sb("before", [P, TT, E, E])
        ties = sb("ties", [P, TT, E, E])
        cum = sb("cum", [P, TT, E])

        th_e = sb("th_e", [P, S])
        sg_e = sb("sg_e", [P, S])
        hf_e = sb("hf_e", [P, S])
        hid_eh = sb("hid_eh", [P, EARLY, IJ, S], F16)
        hid_el = sb("hid_el", [P, EARLY, IJ, S], F16)

        staged = sb("staged", [P, STAGED])
        gu_h = sb("gu_h", [P, EARLY, IJ, WPIECE], F16)
        gu_l = sb("gu_l", [P, EARLY, IJ, WPIECE], F16)
        dn_h = sb("dn_h", [P, EARLY, IJ, D], F16)
        dn_l = sb("dn_l", [P, EARLY, IJ, D], F16)
        hid_h = qst[:, :, :, :].rearrange("p a b c -> p (a b c)").rearrange("p (h j n) -> p h j n", h=2, j=IJ)
        hid_l = kst[:, :, :, :].rearrange("p a b c -> p (a b c)").rearrange("p (h j n) -> p h j n", h=2, j=IJ)
        probv = prob[:, :, :, :, :].rearrange("p a b c d -> p (a b c d)")
        th = [probv[:, 0:TB], probv[:, TB:2 * TB]]
        sg = [probv[:, 2 * TB:3 * TB], probv[:, 3 * TB:4 * TB]]
        hf = [hT[:, :, :].rearrange("p k s -> p (k s)"), q32[:, :, :].rearrange("p k s -> p (k s)")]
        gb_bc = at
        x1f = vx[:, :, :, :, :].rearrange("p a b c d -> p (a b c d)")[:, 0:BT * D].rearrange("p (t d) -> p t d", t=BT)
        fin = vx[:, :, :, :, :].rearrange("p a b c d -> p (a b c d)")[:, BT * D:2 * BT * D].rearrange("p (t d) -> p t d", t=BT)

        accf = acc[:, :, :].rearrange("p t d -> p (t d)")
        o_mod, o_qkv = 0, KD * 6 * D
        o_wo = o_qkv + KD * 3 * D
        o_r = o_wo + KD * D
        o_c = o_r + KD * E
        wmod32 = accf[:, o_mod:o_qkv].rearrange("p (k n) -> p k n", k=KD)
        wq32 = accf[:, o_qkv:o_wo].rearrange("p (k n) -> p k n", k=KD)
        wo32 = accf[:, o_wo:o_r].rearrange("p (k n) -> p k n", k=KD)
        wr32 = accf[:, o_r:o_c].rearrange("p (k n) -> p k n", k=KD)
        c32 = accf[:, o_c:o_c + KD * B].rearrange("p (k n) -> p k n", k=KD)
        staged_gu = staged[:, 0:2 * KD * I].rearrange("p (g n) -> p g n", g=2 * KD)
        staged_dn = staged[:, 2 * KD * I:STAGED]

        q_d = nc.dram_tensor("q_scratch", [2, 2, D, S], F16, kind="Internal").ap()
        k_d = nc.dram_tensor("k_scratch", [2, 2, D, S], F16, kind="Internal").ap()
        x1_d = nc.dram_tensor("residual", [B, S, D], F32, kind="Internal").ap()
        gates_d = nc.dram_tensor("gates_scratch", [2, B, D], F32, kind="Internal").ap()

        names = """c_in wmod_in wqkv_in wo_in bias_in bo_in bias_s_ready ident_ready tanhc_ready siluc_ready mod_done
            modv_ready gr_ready gates_ready gates_out wsplit_h wsplit_l consts_ready pow_ready
            ga_in scr_written st1_ready halves1_ready parts1_ready mv1_ready ve1_ready rs1_ready xn1_ready t1_done hT_ready hh_ready hl_ready
            qp_done q32_ready qh_ready ql_ready kp_done k32_ready kh_ready kl_ready vp_done v_ready
            sc_done max_done nmt_done nm_ready scT_done exp_done pv_done au_ready tn_done rec_ready at_ready
            ta_done aT_ready ah_ready al_ready op_done proj_ready gated_ready x1_ready
            st2_ready halves2_ready parts2_ready mv2_ready ve2_ready rs2_ready xn2_ready t2_done h2T_ready h2h_ready h2l_ready
            rt_done lmax_ready lsh_ready pexp_ready rsum_ready prec_ready rp_ready before_ready ties_ready
            tied_ready joined_ready weighed_ready cum_ready w_ready
            gu_in dn_in wgu_h wgu_l wdn_h wdn_l gu_done th_ready sg_ready hf_ready hidh_ready hidl_ready
            y_done acc_ready gb_in fin_mul fin_add out_done
            gue_done the_ready sge_ready hfe_ready hideh_ready hidel_ready ye_done x1f_in""".split()
        s = {n: sem(n) for n in names}
        x_in = [sem(f"x_in{p}") for p in range(2)]
        stack_in = [sem(f"stack_in{p}") for p in range(2)]
        xr_in = [sem(f"xr_in{p}") for p in range(2)]
        x1_out = [sem(f"x1_out{p}") for p in range(2)]
        nm_in = [sem(f"nm_in{p}") for p in range(2)]

        def passes(w_hi, w_lo, a_hi, a_lo):
            return ((w_hi, a_hi), (w_hi, a_lo), (w_lo, a_hi))

        def run_stage_one(engine, iteration, between={}):
            for n in range(-3, 4):
                if n in between:
                    between[n]()
                iteration(Batch(n // 2, n % 2))
            with engine.Fori(2, (B - 2) // 2) as half:
                iteration(Batch(half, 0))
                iteration(Batch(half, 1))
            for n in range(B - 2, B + 2):
                if n in between:
                    between[n]()
                iteration(Batch(n // 2, n % 2))

        def run_stage_two(engine, step, drain):
            def middle(e):
                with engine.Fori(0, NB // 2 - 1) as m:
                    step(e, 2 * m + 1, 1, before=(e, 2 * m))
                    step(e, 2 * m + 2, 0, before=(e, 2 * m + 1))

            step(0, 0, 0, before=None)
            with engine.Fori(0, LATE - 1) as e:
                middle(e)
                step(e, NB - 1, 1, before=(e, NB - 2), refill_gu=True)
                step(e + 1, 0, 0, before=(e, NB - 1), refill_dn=True)
            middle(LATE - 1)
            step(LATE - 1, NB - 1, 1, before=(LATE - 1, NB - 2))
            drain(LATE - 1, NB - 1, 1)

        block = ctx.enter_context(nc.Block())

        @block.sync
        def _(sp):
            sp.dma_start(c32, c_t.rearrange("(k p) b -> p k b", p=P)).then_inc(s["c_in"], 16)
            sp.dma_start(wmod32, wmod.rearrange("(k p) n -> p k n", p=P)).then_inc(s["wmod_in"], 16)
            sp.dma_start(bias_p[:, :], bqkv_p).then_inc(s["bias_in"], 16)
            sp.dma_start(wq32, wqkv_t.rearrange("(k p) n -> p k n", p=P)).then_inc(s["wqkv_in"], 16)
            sp.dma_start(wo32, wo_t.rearrange("(k p) n -> p k n", p=P)).then_inc(s["wo_in"], 16)
            sp.dma_start(wr32, router_t.rearrange("(k p) n -> p k n", p=P)).then_inc(s["wo_in"], 16)
            sp.dma_start(bo_bc[:, :], b_o.partition_broadcast(P)).then_inc(s["bo_in"], 16)

            def load_expert(e):
                for g, w in enumerate((gate_t, up_t)):
                    sp.dma_start(staged_gu[:, g * KD:(g + 1) * KD, :],
                                 w[bass.ds(e, 1)].rearrange("a (k p) i -> p (a k) i", p=P)).then_inc(s["gu_in"], 16)
                sp.dma_start(staged_dn.rearrange("p (j d) -> p j d", j=IJ),
                             down_t[bass.ds(e, 1)].rearrange("a (j p) d -> p (a j) d", p=P)).then_inc(s["dn_in"], 16)

            def store_gates():
                wait(sp, s["gates_ready"], 2)
                sp.dma_start(gates_d.rearrange("g b d -> b g d"), gate_r[:, :, :]).then_inc(s["gates_out"], 16)
                wait(sp, s["consts_ready"], 4)
                load_expert(0)

            def iteration(c):
                n, o, ahead = c.at(1), c.at(-1), c.at(2)
                if ahead.real:
                    wait(sp, s["xn1_ready"], TT * (ahead.n - 1))
                    sp.dma_start(xa[:, ahead.par, :, :],
                                 x[bass.ds(ahead.n, 1)].rearrange("a (t p) d -> p (a t) d", p=P)).then_inc(x_in[ahead.par], 16)
                if n.real:
                    wait(sp, stack_in[n.par], 12 * 16 * n.half)
                    wait(sp, s["qh_ready"], n.n + 1)
                    wait(sp, s["ql_ready"], n.n + 1)
                    for part, src in enumerate((qh, ql)):
                        sp.dma_start(q_d[n.par, part].rearrange("(k p) s -> p k s", p=P), src[:, :, :]).then_inc(s["scr_written"], 16)
                if c.real:
                    wait(sp, x1_out[c.par], 16 * c.half)
                    wait(sp, s["xn2_ready"], TT * c.n - TT)
                    sp.dma_start(xr[:, c.par, :, :],
                                 x[bass.ds(c.n, 1)].rearrange("a (t p) d -> p (a t) d", p=P)).then_inc(xr_in[c.par], 16)
                    wait(sp, s["nm_ready"], c.n + 1)
                    for odd in range(2):
                        sp.dma_start(qst[64 * odd + STACK:64 * odd + STACK + 1, c.par, :, :],
                                     nm[PAIRS * odd:PAIRS * (odd + 1), :]).then_inc(nm_in[c.par], 16)
                if n.real:
                    wait(sp, s["kh_ready"], n.n + 1)
                    wait(sp, s["kl_ready"], n.n + 1)
                    for part, src in enumerate((kh, kl)):
                        sp.dma_start(k_d[n.par, part].rearrange("(k p) s -> p k s", p=P), src[:, :, :]).then_inc(s["scr_written"], 16)
                    wait(sp, s["scr_written"], 64 * (n.n + 1))
                    wait(sp, s["scT_done"], PAIRS * n.n - PAIRS)
                    for odd in range(2):
                        for r, (qpart, kpart) in enumerate(((0, 0), (0, 1), (1, 0))):
                            row = 64 * odd + HD * r
                            for stack, scratch, part in ((qst, q_d, qpart), (kst, k_d, kpart)):
                                src = scratch[n.par, part].rearrange("(s o d) t -> o d s t", o=2, d=HD)[odd]
                                sp.dma_start(stack[row:row + HD, n.par, :, :], src).then_inc(stack_in[n.par], 16)
                if o.real:
                    wait(sp, s["x1_ready"], o.n + 1)
                    sp.dma_start(x1_d[bass.ds(o.n, 1)].rearrange("a (t p) d -> p (a t) d", p=P),
                                 xr[:, o.par, :, :]).then_inc(x1_out[o.par], 16)
                if c.real:
                    if isinstance(c.n, int) and c.n == 0:
                        wait(sp, s["gates_out"], 16)
                    wait(sp, s["gated_ready"], c.n)
                    sp.dma_start(ga_bc[:, :], gates_d[0, bass.ds(c.n, 1), :].rearrange("a d -> (a d)").partition_broadcast(P)).then_inc(s["ga_in"], 16)

            def load_next(e):
                wait(sp, s["wgu_h"], IJ * e)
                wait(sp, s["wgu_l"], IJ * e)
                wait(sp, s["wdn_h"], e)
                wait(sp, s["wdn_l"], e)
                load_expert(e)

            run_stage_one(sp, iteration, {-1: store_gates, 1: lambda: load_next(1), B - 2: lambda: load_next(2)})

            with sp.Fori(EARLY + 1, E) as e:
                load_next(e)
            for p in range(2):
                wait(sp, x1_out[p], 16 * B // 2)

            def finish(blk):
                sp.dma_start(gb_bc[:, :, :].rearrange("p b d -> p (b d)"),
                             gates_d[1, bass.ds(2 * blk, 2), :].rearrange("b d -> (b d)").partition_broadcast(P)).then_inc(s["gb_in"], 16)
                sp.dma_start(x1f, x1_d[bass.ds(2 * blk, 2)].rearrange("b (t p) d -> p (b t) d", p=P)).then_inc(s["x1f_in"], 16)
                wait(sp, s["fin_add"], blk + 1)
                sp.dma_start(out[bass.ds(2 * blk, 2)].rearrange("b (t p) d -> p (b t) d", p=P),
                             fin).then_inc(s["out_done"], 16)

            with sp.Fori(0, NB) as blk:
                finish(blk)
            wait(sp, s["out_done"], 16 * NB)

        @block.gpsimd
        def _(pool):
            pool.memset(ident[:, :], 0.0).then_inc(s["ident_ready"], 1)
            pool.wait_ge(s["ident_ready"], 1)
            pool.affine_select(out=ident[:, :], in_=ident[:, :], compare_op=ALU.not_equal, fill=1.0, base=0,
                               pattern=[[-1, P]], channel_multiplier=1).then_inc(s["ident_ready"], 1)
            pool.memset(halfpow[:, :], -0.5).then_inc(s["pow_ready"], 1)
            pool.memset(eps[:, :], EPS).then_inc(s["pow_ready"], 1)
            pool.wait_ge(s["pow_ready"], 2)
            pool.memset(earlier[:, :, :], 1.0).then_inc(s["consts_ready"], 1)
            pool.wait_ge(s["consts_ready"], 1)
            pool.affine_select(out=earlier[:, :, :], in_=earlier[:, :, :], compare_op=ALU.is_gt, fill=0.0, base=0,
                               pattern=[[1, E], [-1, E]], channel_multiplier=0).then_inc(s["consts_ready"], 1)
            pool.memset(kst[:, :, :, :].rearrange("p a b c -> p (a b c)"), MAXK).then_inc(s["consts_ready"], 1)
            pool.memset(vx[:, :, :, :, :].rearrange("p a b c d -> p (a b c d)"), 1.0).then_inc(s["consts_ready"], 1)

            def clear_acc():
                pool.wait_ge(s["mod_done"], 2)
                pool.wait_ge(s["siluc_ready"], 1)
                pool.wait_ge(s["wsplit_h"], 3)
                pool.wait_ge(s["wsplit_l"], 3)
                for q in range(CLEARED):
                    pool.memset(acc[:, q * NT // CLEARED:(q + 1) * NT // CLEARED, :].rearrange("p t d -> p (t d)"), 0.0).then_inc(s["acc_ready"], 1)

            def inverse_deviation(mv, ve, rs, mv_sem, ve_sem, rs_sem, n):
                pool.wait_ge(s[mv_sem], TT * (n + 1))
                pool.tensor_tensor(ve[:, :], mv[:, :, 1], eps[:, :], ALU.add).then_inc(s[ve_sem], 1)
                pool.wait_ge(s[ve_sem], n + 1)
                pool.tensor_tensor(rs[:, :], ve[:, :], halfpow[:, :], ALU.pow).then_inc(s[rs_sem], 1)

            def hidden_low(a, i):
                if a.real:
                    wait(pool, s["hideh_ready"], CHUNKS * a.n + i + 1)
                    pool.tensor_tensor(hid_el[:, i // IJ, i % IJ, :], hf_e[:, :], hid_eh[:, i // IJ, i % IJ, :],
                                       ALU.subtract).then_inc(s["hidel_ready"], 1)

            def iteration(c):
                n, o, a, m = c.at(1), c.at(-1), c.at(-2), c.at(2)
                hidden_low(a, 0)
                if n.real:
                    wait(pool, s["hh_ready"], n.n + 1)
                    wait(pool, s["vp_done"], n.n)
                    pool.tensor_tensor(hl[:, :, :], hT[:, :, :], hh[:, :, :], ALU.subtract).then_inc(s["hl_ready"], 1)
                hidden_low(a, 1)
                if n.real:
                    wait(pool, s["qh_ready"], n.n + 1)
                    pool.tensor_tensor(ql[:, :, :], q32[:, :, :], qh[:, :, :], ALU.subtract).then_inc(s["ql_ready"], 1)
                    wait(pool, s["kh_ready"], n.n + 1)
                    wait(pool, s["scr_written"], 64 * n.n)
                    pool.tensor_tensor(kl[:, :, :], k32[:, :, :], kh[:, :, :], ALU.subtract).then_inc(s["kl_ready"], 1)
                hidden_low(a, 2)
                if o.real:
                    wait(pool, s["ah_ready"], o.n + 1)
                    pool.tensor_tensor(al[:, :, :], aT[:, :, :], ah[:, :, :], ALU.subtract).then_inc(s["al_ready"], 1)
                hidden_low(a, 3)
                hidden_low(a, 4)
                if o.real:
                    wait(pool, s["proj_ready"], o.n + 1)
                    wait(pool, s["ga_in"], 16 * (o.n + 1))
                    pool.tensor_tensor(gated[:, :, :], proj[:, :, :], ga_bc[:, :].unsqueeze(1).to_broadcast([P, TT, D]),
                                       ALU.mult).then_inc(s["gated_ready"], 1)
                    wait(pool, s["gated_ready"], o.n + 1)
                    wait(pool, xr_in[o.par], 16 * (o.half + 1))
                    tile = xr[:, o.par, :, :]
                    pool.tensor_tensor(tile, tile, gated[:, :, :], ALU.add).then_inc(s["x1_ready"], 1)
                hidden_low(a, 5)
                if o.real:
                    inverse_deviation(mv2, ve2, rs2, "mv2_ready", "ve2_ready", "rs2_ready", o.n)
                if m.real:
                    inverse_deviation(mv1, ve1, rs1, "mv1_ready", "ve1_ready", "rs1_ready", m.n)
                hidden_low(a, 6)
                hidden_low(a, 7)

            run_stage_one(pool, iteration, {0: clear_acc})

            def finish(blk):
                pool.wait_ge(s["acc_ready"], CLEARED + BT * (NB * (E - 1) + blk + 1))
                pool.wait_ge(s["gb_in"], 16 * (blk + 1))
                wait(pool, s["out_done"], 16 * blk)
                for b in range(2):
                    pool.tensor_tensor(fin[:, TT * b:TT * (b + 1), :], acc[:, bass.ds(BT * blk + TT * b, TT), :],
                                       gb_bc[:, b, :].unsqueeze(1).to_broadcast([P, TT, D]), ALU.mult).then_inc(s["fin_mul"], 1)
                pool.wait_ge(s["x1f_in"], 16 * (blk + 1))
                pool.wait_ge(s["fin_mul"], 2 * (blk + 1))
                pool.tensor_tensor(fin, fin, x1f, ALU.add).then_inc(s["fin_add"], 1)

            finish(0)
            with pool.Fori(1, NB) as blk:
                finish(blk)

        @block.scalar
        def _(act):
            act.wait_ge(s["c_in"], 16)
            act.activation(tanh_c[:, :, :], c32, ACT.Tanh, scale=0.5).then_inc(s["tanhc_ready"], 1)
            act.wait_ge(s["wqkv_in"], 16)
            act.activation(wq_h[:, :, :], wq32, ACT.Copy, scale=WS).then_inc(s["wsplit_h"], 1)
            act.wait_ge(s["wo_in"], 32)
            act.activation(wo_h[:, :, :], wo32, ACT.Copy, scale=WS).then_inc(s["wsplit_h"], 1)
            act.activation(wr_h[:, :, :], wr32, ACT.Copy, scale=WS).then_inc(s["wsplit_h"], 1)

            def modulated(dst, src, norm, n, done):
                for k in range(KD):
                    act.activation(dst[:, k, :], src[:, k, :], ACT.Identity, scale=modv[:, 2 * norm + 1, k, bass.ds(n, 1)],
                                   bias=modv[:, 2 * norm, k, bass.ds(n, 1)]).then_inc(s[done], 1)

            def tanh_piece(a, i):
                if a.real:
                    wait(act, s["gue_done"], CHUNKS * a.n + i + 1)
                    wait(act, s["sge_ready"], CHUNKS * a.n + i)
                    act.activation(th_e[:, :], bank[:, 5, 0:S], ACT.Tanh, scale=0.5 / GU_SCALE).then_inc(s["the_ready"], 1)

            def hidden_high(a, i):
                if a.real:
                    wait(act, s["hfe_ready"], CHUNKS * a.n + i + 1)
                    wait(act, s["ye_done"], TT * EARLY * a.n)
                    act.activation(hid_eh[:, i // IJ, i % IJ, :], hf_e[:, :], ACT.Copy).then_inc(s["hideh_ready"], 1)

            def iteration(c):
                n, o, a = c.at(1), c.at(-1), c.at(-2)
                misc = [bank[:, 6 + i, :].rearrange("p (k s) -> p k s", k=2) for i in range(2)]

                def exponentials(pair):
                    if c.real:
                        wait(act, s["scT_done"], PAIRS * c.n + pair + 1)
                        wait(act, s["pv_done"], PAIRS * c.n + pair - 1)
                        r = 2 * (pair % 2)
                        act.activation(prob[:, pair % 2, :, :, :].rearrange("p a b c -> p (a b c)"),
                                       bank[:, r:r + 2, :].rearrange("p a b -> p (a b)"),
                                       ACT.Exp, scale=1.0 / SS).then_inc(s["exp_done"], 1)

                def sums(half):
                    if c.real:
                        wait(act, s["pv_done"], PAIRS * c.n + 4 * (half + 1))
                        wait(act, s["tn_done"], TT * c.n)
                        act.activation(au[:, 2 * half:2 * half + 2, :].rearrange("p g s -> p (g s)"), bank[:, 4, :],
                                       ACT.Copy).then_inc(s["au_ready"], 1)

                tanh_piece(a, 0)
                if n.real:
                    if isinstance(n.n, int) and n.n == 0:
                        act.wait_ge(s["modv_ready"], 2)
                        act.wait_ge(s["bias_s_ready"], 3)
                    wait(act, s["t1_done"], n.n + 1)
                    wait(act, s["hl_ready"], n.n)
                    modulated(hT, misc[0], 0, n.n, "hT_ready")
                    wait(act, s["hT_ready"], 2 * (n.n + 1))
                    wait(act, s["vp_done"], n.n)
                    act.activation(hh[:, :, :], hT[:, :, :], ACT.Copy).then_inc(s["hh_ready"], 1)
                hidden_high(a, 0)
                tanh_piece(a, 1)
                hidden_high(a, 1)
                if n.real:
                    wait(act, s["qp_done"], n.n + 1)
                    wait(act, s["ql_ready"], n.n)
                    for m in range(2):
                        act.activation(q32[:, m, :], misc[1][:, m, :], ACT.Identity, scale=QS / GU_SCALE,
                                       bias=bias_s[:, m:m + 1]).then_inc(s["q32_ready"], 1)
                    wait(act, s["q32_ready"], 2 * (n.n + 1))
                    wait(act, s["scr_written"], 64 * n.n)
                    act.activation(qh[:, :, :], q32[:, :, :], ACT.Copy).then_inc(s["qh_ready"], 1)
                tanh_piece(a, 2)
                if n.real:
                    wait(act, s["kp_done"], n.n + 1)
                    wait(act, s["kl_ready"], n.n)
                    for m in range(2):
                        act.activation(k32[:, m, :], misc[0][:, m, :], ACT.Identity, scale=XS / GU_SCALE,
                                       bias=bias_s[:, 2 + m:3 + m]).then_inc(s["k32_ready"], 1)
                    wait(act, s["k32_ready"], 2 * (n.n + 1))
                    act.activation(kh[:, :, :], k32[:, :, :], ACT.Copy).then_inc(s["kh_ready"], 1)
                hidden_high(a, 2)
                if o.real:
                    wait(act, s["ta_done"], o.n + 1)
                    wait(act, s["al_ready"], o.n)
                    for k in range(KD):
                        act.activation(aT[:, k, :], misc[1][:, k, :], ACT.Identity, scale=XS,
                                       bias=bias_s[:, 4 + k:5 + k]).then_inc(s["aT_ready"], 1)
                    wait(act, s["aT_ready"], 2 * (o.n + 1))
                    wait(act, s["op_done"], o.n)
                    act.activation(ah[:, :, :], aT[:, :, :], ACT.Copy).then_inc(s["ah_ready"], 1)
                tanh_piece(a, 3)
                if n.real:
                    wait(act, s["vp_done"], n.n + 1)
                    wait(act, s["pv_done"], PAIRS * (n.n - 1))
                    if isinstance(n.n, int) and n.n < 2:
                        act.wait_ge(s["consts_ready"], 4)
                    for t in range(TT):
                        act.activation(vx[:, n.par, t, :, 0:HD], misc[0][:, t, :].rearrange("p (h d) -> p h d", h=H),
                                       ACT.Copy, scale=1.0 / GU_SCALE).then_inc(s["v_ready"], 1)
                hidden_high(a, 3)
                tanh_piece(a, 4)
                hidden_high(a, 4)
                tanh_piece(a, 5)
                hidden_high(a, 5)
                exponentials(0)
                tanh_piece(a, 6)
                exponentials(1)
                exponentials(2)
                hidden_high(a, 6)
                exponentials(3)
                tanh_piece(a, 7)
                exponentials(4)
                hidden_high(a, 7)
                sums(0)
                exponentials(5)
                if o.real:
                    wait(act, s["t2_done"], o.n + 1)
                    wait(act, s["h2l_ready"], o.n)
                    modulated(h2T, misc[1], 1, o.n, "h2T_ready")
                exponentials(6)
                if o.real:
                    wait(act, s["h2T_ready"], 2 * (o.n + 1))
                    act.activation(h2h[:, :, bass.ds(S * o.n, S)], h2T[:, :, :], ACT.Copy).then_inc(s["h2h_ready"], 1)
                exponentials(7)
                sums(1)
                if o.real:
                    wait(act, s["lsh_ready"], o.n + 1)
                    wait(act, s["rp_ready"], o.n)
                    act.activation(pexp[:, :, :], lsh[:, :, :], ACT.Exp, scale=1.0 / GU_SCALE).then_inc(s["pexp_ready"], 1)

            def split_gu(place, j):
                act.activation(gu_h[:, place, j, :].rearrange("p (g m) -> p g m", g=2 * KD), staged_gu[:, :, j * P:(j + 1) * P],
                               ACT.Copy, scale=WS).then_inc(s["wgu_h"], 1)

            def split_dn(place, e):
                act.wait_ge(s["dn_in"], 16 * (e + 1))
                act.activation(dn_h[:, place, :, :].rearrange("p j d -> p (j d)"), staged_dn, ACT.Copy, scale=WS).then_inc(s["wdn_h"], 1)

            def split_early(e):
                act.wait_ge(s["gu_in"], 32 * (e + 1))
                for j in range(IJ):
                    split_gu(e, j)
                split_dn(e, e)

            run_stage_one(act, iteration, {0: lambda: split_early(0), 2: lambda: split_early(1)})

            def step(e, blk, par, before, refill_gu=False, refill_dn=False):
                done = IJ * (NB * e + blk)
                for j in range(IJ):
                    wait(act, s["gu_done"], done + j + 1)
                    wait(act, s["sg_ready"], done + j - 1)
                    act.activation(th[j % 2], bank[:, 2 * (j % 2), :], ACT.Tanh, scale=0.5 / GU_SCALE).then_inc(s["th_ready"], 1)
                    wait(act, s["hf_ready"], done + j + 1)
                    act.activation(hid_h[:, par, j, :], hf[j % 2], ACT.Copy).then_inc(s["hidh_ready"], 1)
                    if refill_gu:
                        if j == 0:
                            act.wait_ge(s["gu_in"], 32 * (EARLY + e + 2))
                        split_gu(0, j)
                if refill_dn:
                    wait(act, s["y_done"], BT * NB * e)
                    split_dn(0, EARLY + e)

            act.wait_ge(s["gu_in"], 32 * (EARLY + 1))
            act.wait_ge(s["gue_done"], CHUNKS * (B - 1) + IJ)
            for j in range(IJ):
                split_gu(0, j)
            act.wait_ge(s["ye_done"], TT * (EARLY * (B - 1) + 1))
            split_dn(0, EARLY)
            run_stage_two(act, step, lambda e, blk, par: None)

        @block.vector
        def _(dve):
            dve.wait_ge(s["tanhc_ready"], 1)
            dve.scalar_tensor_tensor(out=silu_c[:, :, :], in0=tanh_c[:, :, :], scalar=1.0, in1=c32,
                                     op0=ALU.add, op1=ALU.mult).then_inc(s["siluc_ready"], 1)
            dve.wait_ge(s["bias_in"], 16)
            for first, scale in ((0, QS), (2, XS), (4, XS)):
                dve.tensor_scalar(bias_s[:, first:first + 2], bias_p[:, first:first + 2], scale, None,
                                  ALU.mult).then_inc(s["bias_s_ready"], 1)
            dve.wait_ge(s["mod_done"], 1)
            made = bank[:, 6, 0:4 * KD * B].rearrange("p (l w n) -> p l w n", l=2, w=2)
            kept = modv[:, :, :, :].rearrange("p (l w) k b -> p l w (k b)", w=2)
            dve.tensor_scalar(kept[:, :, 0, :], made[:, :, 0, :], XS / 2, None, ALU.mult).then_inc(s["modv_ready"], 1)
            dve.tensor_scalar(kept[:, :, 1, :], made[:, :, 1, :], XS / 2, XS, ALU.mult, ALU.add).then_inc(s["modv_ready"], 1)
            dve.wait_ge(s["mod_done"], 2)
            rows = bank[0:B, 7, :].rearrange("b (g d) -> b g d", g=2)
            dve.tensor_scalar(gate_r[:, :, :], rows, 0.5, None, ALU.mult).then_inc(s["gr_ready"], 1)
            dve.wait_ge(s["gr_ready"], 1)
            dve.tensor_scalar(gate_s[:, :, :], gate_r[:, :, :], 0.0, 2.0, ALU.is_ge, ALU.mult).then_inc(s["gr_ready"], 1)
            dve.wait_ge(s["gr_ready"], 2)
            dve.scalar_tensor_tensor(out=gate_m[:, :, :], in0=gate_s[:, :, :], scalar=-1.0, in1=gate_r[:, :, :],
                                     op0=ALU.add, op1=ALU.mult).then_inc(s["gr_ready"], 1)
            dve.wait_ge(s["gr_ready"], 3)
            for g, scale in enumerate((1.0, 1.0 / WS)):
                dve.tensor_scalar(gate_m[:, g, :], gate_m[:, g, :], GATE_MIN, scale, ALU.max, ALU.mult).then_inc(s["gr_ready"], 1)
            dve.wait_ge(s["gr_ready"], 5)
            for g in range(2):
                dve.scalar_tensor_tensor(out=gate_r[:, g, :], in0=gate_s[:, g, :], scalar=-1.0, in1=gate_m[:, g, :],
                                         op0=ALU.add, op1=ALU.mult).then_inc(s["gates_ready"], 1)
            for count, (lo, full, hi) in enumerate(((wq_l, wq32, wq_h), (wo_l, wo32, wo_h), (wr_l, wr32, wr_h))):
                dve.wait_ge(s["wsplit_h"], count + 1)
                dve.scalar_tensor_tensor(out=lo[:, :, :], in0=full, scalar=WS, in1=hi[:, :, :],
                                         op0=ALU.mult, op1=ALU.subtract).then_inc(s["wsplit_l"], 1)
            dve.wait_ge(s["consts_ready"], 2)
            dve.wait_ge(s["bo_in"], 16)

            def statistics(stats, parts, mv, of, src, n):
                stats_sem, halves_sem, parts_sem, mv_sem = (s[f"{name}{of}_ready"] for name in ("st", "halves", "parts", "mv"))
                for t in range(TT):
                    dve.bn_stats(stats[:, t, :], src[:, t, :]).then_inc(stats_sem, 1)
                wait(dve, stats_sem, TT * (n + 1))
                even, odd = stats[:, :, 1:3], stats[:, :, 4:6]
                total, apart, apart2 = parts[:, :, 0:2], parts[:, :, 2], parts[:, :, 3]
                dve.tensor_tensor(total, even, odd, ALU.add).then_inc(halves_sem, 1)
                dve.tensor_tensor(apart, even[:, :, 0], odd[:, :, 0], ALU.subtract).then_inc(halves_sem, 1)
                wait(dve, halves_sem, 2 * (n + 1))
                dve.scalar_tensor_tensor(out=apart2, in0=apart, scalar=0.25, in1=apart, op0=ALU.mult, op1=ALU.mult).then_inc(parts_sem, 1)
                dve.tensor_scalar(mv[:, :, 0], total[:, :, 0], 0.5, None, ALU.mult).then_inc(mv_sem, 1)
                wait(dve, parts_sem, n + 1)
                dve.scalar_tensor_tensor(out=mv[:, :, 1], in0=total[:, :, 1], scalar=1.0 / D, in1=apart2,
                                         op0=ALU.mult, op1=ALU.add).then_inc(mv_sem, 1)

            def normalise(xn, mv, rs, done, src):
                for t in range(TT):
                    dve.tensor_scalar(xn[:, t, :], src[:, t, :], mv[:, t, 0:1], rs[:, t:t + 1], ALU.subtract, ALU.mult).then_inc(s[done], 1)

            def route_logits(o):
                wait(dve, s["rt_done"], o.n + 1)
                logits = bank[:, 6, 0:TT * E].rearrange("p (t e) -> p t e", t=TT)
                dve.tensor_reduce(lmax[:, :], logits, AX.X, ALU.max).then_inc(s["lmax_ready"], 1)
                wait(dve, s["lmax_ready"], o.n + 1)
                dve.tensor_tensor(lsh[:, :, :], logits, lmax[:, :].unsqueeze(2).to_broadcast([P, TT, E]),
                                  ALU.subtract).then_inc(s["lsh_ready"], 1)

            mine = rp[:, :, :].unsqueeze(3).to_broadcast([P, TT, E, E])
            other = rp[:, :, :].unsqueeze(2).to_broadcast([P, TT, E, E])

            def route_sum(a):
                wait(dve, s["pexp_ready"], a.n + 1)
                dve.tensor_reduce(psum_r[:, :], pexp[:, :, :], AX.X, ALU.add).then_inc(s["rsum_ready"], 1)
                wait(dve, s["rsum_ready"], a.n + 1)
                dve.reciprocal(prec[:, :], psum_r[:, :]).then_inc(s["prec_ready"], 1)

            def route_probabilities(a):
                wait(dve, s["prec_ready"], a.n + 1)
                dve.tensor_tensor(rp[:, :, :], pexp[:, :, :], prec[:, :].unsqueeze(2).to_broadcast([P, TT, E]),
                                  ALU.mult).then_inc(s["rp_ready"], 1)

            def route_order(a):
                wait(dve, s["rp_ready"], a.n + 1)
                dve.tensor_tensor(ties[:, :, :, :], other, mine, ALU.is_equal).then_inc(s["ties_ready"], 1)
                dve.tensor_tensor(before[:, :, :, :], other, mine, ALU.is_gt).then_inc(s["before_ready"], 1)
                wait(dve, s["ties_ready"], a.n + 1)
                dve.tensor_tensor(ties[:, :, :, :], ties[:, :, :, :], earlier[:, :, :].unsqueeze(1).to_broadcast([P, TT, E, E]),
                                  ALU.mult).then_inc(s["tied_ready"], 1)

            def route_join(a):
                wait(dve, s["before_ready"], a.n + 1)
                wait(dve, s["tied_ready"], a.n + 1)
                dve.tensor_tensor(before[:, :, :, :], before[:, :, :, :], ties[:, :, :, :], ALU.add).then_inc(s["joined_ready"], 1)

            def route_weigh(a):
                wait(dve, s["joined_ready"], a.n + 1)
                dve.tensor_tensor(ties[:, :, :, :], before[:, :, :, :], other, ALU.mult).then_inc(s["weighed_ready"], 1)

            def route_cumulate(a):
                wait(dve, s["weighed_ready"], a.n + 1)
                dve.tensor_reduce(cum[:, :, :], ties[:, :, :, :], AX.X, ALU.add).then_inc(s["cum_ready"], 1)

            def route_weights(a):
                wait(dve, s["cum_ready"], a.n + 1)
                dve.scalar_tensor_tensor(out=wts[:, bass.ds(TT * a.n, TT), :], in0=cum[:, :, :], scalar=TOP_P, in1=rp[:, :, :],
                                         op0=ALU.is_le, op1=ALU.mult).then_inc(s["w_ready"], 1)

            def gated_piece(a, i):
                if a.real:
                    wait(dve, s["the_ready"], CHUNKS * a.n + i + 1)
                    dve.scalar_tensor_tensor(out=sg_e[:, :], in0=th_e[:, :], scalar=1.0, in1=bank[:, 5, 0:S],
                                             op0=ALU.add, op1=ALU.mult).then_inc(s["sge_ready"], 1)
                    wait(dve, s["sge_ready"], CHUNKS * a.n + i + 1)
                    wait(dve, s["hidel_ready"], CHUNKS * a.n + i)
                    dve.scalar_tensor_tensor(out=hf_e[:, :], in0=sg_e[:, :], scalar=0.5 / GU_SCALE ** 2,
                                             in1=bank[:, 5, S:2 * S], op0=ALU.mult, op1=ALU.mult).then_inc(s["hfe_ready"], 1)

            def early_share(a, e):
                if a.real:
                    wait(dve, s["w_ready"], a.n + 1)
                    wait(dve, s["ye_done"], TT * (EARLY * a.n + e + 1))
                    for t in range(TT):
                        tile = acc[:, bass.ds(TT * a.n + t, 1), :].rearrange("p a d -> p (a d)")
                        dve.scalar_tensor_tensor(out=tile, in0=bank[:, 7, t * D:(t + 1) * D],
                                                 scalar=wts[:, bass.ds(TT * a.n + t, 1), e:e + 1].rearrange("p a b -> p (a b)"),
                                                 in1=tile, op0=ALU.mult, op1=ALU.add).then_inc(s["acc_ready"], 1)

            def iteration(c):
                n, o, a, m = c.at(1), c.at(-1), c.at(-2), c.at(2)

                def maxima(c, pair):
                    if not c.real:
                        return
                    wait(dve, s["sc_done"], PAIRS * c.n + pair + 1)
                    if pair == 0:
                        wait(dve, s["nmt_done"], c.n)
                    r = 2 * (pair % 2)
                    dve.tensor_reduce(mx[:, :, :, pair].rearrange("p t o -> p o t"),
                                      bank[:, r:r + 2, :].rearrange("p o (t s) -> p o t s", t=TT),
                                      AX.X, ALU.max).then_inc(s["max_done"], 1)

                def route(*steps):
                    if a.real:
                        for step in steps:
                            step(a)

                route(route_sum)
                gated_piece(a, 0)
                route(route_probabilities)
                maxima(c, 2)
                if o.real:
                    wait(dve, s["ta_done"], o.n)
                    for t in range(TT):
                        heads = bank[:, 7 - t, :].rearrange("p (h w) -> p h w", h=H)
                        wait(dve, s["tn_done"], TT * o.n + t + 1)
                        dve.reciprocal(rec[:, t, :], heads[:, :, HD]).then_inc(s["rec_ready"], 1)
                    for t in range(TT):
                        heads = bank[:, 7 - t, :].rearrange("p (h w) -> p h w", h=H)
                        wait(dve, s["rec_ready"], TT * o.n + t + 1)
                        dve.tensor_tensor(at[:, t, :].rearrange("p (h d) -> p h d", h=H), heads[:, :, 0:HD],
                                          rec[:, t, :].unsqueeze(2).to_broadcast([P, H, HD]), ALU.mult).then_inc(s["at_ready"], 1)
                gated_piece(a, 1)
                maxima(c, 3)
                route(route_order)
                maxima(c, 4)
                route(route_join)
                gated_piece(a, 2)
                route(route_weigh)
                maxima(c, 5)
                route(route_cumulate)
                gated_piece(a, 3)
                route(route_weights)
                maxima(c, 6)
                gated_piece(a, 4)
                maxima(c, 7)
                if c.real:
                    wait(dve, s["nmt_done"], c.n + 1)
                    wait(dve, nm_in[1 - c.par], 32 * (c.at(-1).half + 1))
                    dve.tensor_scalar(nm[:, :], bank[0:H, 7, 0:S], -1.0 / MAXK, None, ALU.mult).then_inc(s["nm_ready"], 1)
                if o.real:
                    wait(dve, s["op_done"], o.n + 1)
                    wait(dve, s["gated_ready"], o.n)
                    dve.scalar_tensor_tensor(out=proj[:, :, :], in0=bank[:, 6, :].rearrange("p (t d) -> p t d", t=TT),
                                             scalar=1.0 / GU_SCALE, in1=bo_bc[:, :].unsqueeze(1).to_broadcast([P, TT, D]),
                                             op0=ALU.mult, op1=ALU.add).then_inc(s["proj_ready"], 1)
                gated_piece(a, 5)
                if m.real:
                    wait(dve, x_in[m.par], 16 * (m.half + 1))
                    statistics(bn1, parts1, mv1, 1, xa[:, m.par, :, :], m.n)
                early_share(a, 0)
                gated_piece(a, 6)
                if o.real:
                    wait(dve, s["x1_ready"], o.n + 1)
                    statistics(bn2, parts2, mv2, 2, xr[:, o.par, :, :], o.n)
                gated_piece(a, 7)
                if o.real:
                    wait(dve, s["rs2_ready"], o.n + 1)
                    normalise(xn2, mv2, rs2, "xn2_ready", xr[:, o.par, :, :])
                if m.real:
                    wait(dve, s["rs1_ready"], m.n + 1)
                    wait(dve, s["t1_done"], m.n)
                    normalise(xn1, mv1, rs1, "xn1_ready", xa[:, m.par, :, :])
                if o.real:
                    wait(dve, s["h2h_ready"], o.n + 1)
                    dve.tensor_tensor(h2l[:, :, bass.ds(S * o.n, S)], h2T[:, :, :], h2h[:, :, bass.ds(S * o.n, S)],
                                      ALU.subtract).then_inc(s["h2l_ready"], 1)
                maxima(n, 0)
                maxima(n, 1)
                early_share(a, 1)
                if o.real:
                    route_logits(o)

            def split_gu(place, count, j):
                dve.wait_ge(s["wgu_h"], count)
                dve.scalar_tensor_tensor(out=gu_l[:, place, j, :].rearrange("p (g m) -> p g m", g=2 * KD),
                                         in0=staged_gu[:, :, j * P:(j + 1) * P], scalar=WS,
                                         in1=gu_h[:, place, j, :].rearrange("p (g m) -> p g m", g=2 * KD),
                                         op0=ALU.mult, op1=ALU.subtract).then_inc(s["wgu_l"], 1)

            def split_dn(place, e):
                dve.wait_ge(s["wdn_h"], e + 1)
                dve.scalar_tensor_tensor(out=dn_l[:, place, :, :].rearrange("p j d -> p (j d)"), in0=staged_dn, scalar=WS,
                                         in1=dn_h[:, place, :, :].rearrange("p j d -> p (j d)"),
                                         op0=ALU.mult, op1=ALU.subtract).then_inc(s["wdn_l"], 1)

            def split_expert(place, e):
                for j in range(IJ):
                    split_gu(place, IJ * e + j + 1, j)
                split_dn(place, e)

            run_stage_one(dve, iteration, {0: lambda: split_expert(0, 0), 2: lambda: split_expert(1, 1)})

            def add_share(e, blk, t):
                done = BT * (NB * e + blk) + t
                wait(dve, s["y_done"], done + 1)
                tile = acc[:, bass.ds(BT * blk + t, 1), :].rearrange("p a d -> p (a d)")
                dve.scalar_tensor_tensor(out=tile, in0=bank[:, 4 + t, 0:D],
                                         scalar=wts[:, bass.ds(BT * blk + t, 1), bass.ds(EARLY + e, 1)].rearrange("p a b -> p (a b)"),
                                         in1=tile, op0=ALU.mult, op1=ALU.add).then_inc(s["acc_ready"], 1)

            def step(e, blk, par, before, refill_gu=False, refill_dn=False):
                done = IJ * (NB * e + blk)
                for j in range(IJ):
                    wait(dve, s["th_ready"], done + j + 1)
                    dve.scalar_tensor_tensor(out=sg[j % 2], in0=th[j % 2], scalar=1.0, in1=bank[:, 2 * (j % 2), :],
                                             op0=ALU.add, op1=ALU.mult).then_inc(s["sg_ready"], 1)
                    wait(dve, s["sg_ready"], done + j + 1)
                    dve.scalar_tensor_tensor(out=hf[j % 2], in0=sg[j % 2], scalar=0.5 / GU_SCALE ** 2,
                                             in1=bank[:, 2 * (j % 2) + 1, :], op0=ALU.mult, op1=ALU.mult).then_inc(s["hf_ready"], 1)
                    if before is not None:
                        add_share(*before, j)
                    wait(dve, s["hidh_ready"], done + j + 1)
                    dve.tensor_tensor(hid_l[:, par, j, :], hf[j % 2], hid_h[:, par, j, :], ALU.subtract).then_inc(s["hidl_ready"], 1)
                    if refill_gu:
                        split_gu(0, IJ * (EARLY + e + 1) + j + 1, j)
                if refill_dn:
                    split_dn(0, EARLY + e)

            def drain(e, blk, par):
                for t in range(BT):
                    add_share(e, blk, t)

            split_expert(0, EARLY)
            run_stage_two(dve, step, drain)

        @block.tensor
        def _(pe):
            pe.wait_ge(s["siluc_ready"], 1)
            pe.wait_ge(s["wmod_in"], 16)
            for q, col in enumerate((0, 1, 3, 4)):
                for m in range(KD):
                    at_col = (q * KD + m) * B
                    for k in range(KD):
                        mm = pe.matmul(bank[:, 6, at_col:at_col + B], wmod32[:, k, col * D + m * P:col * D + (m + 1) * P],
                                       silu_c[:, k, :], start=(k == 0), stop=(k == KD - 1))
            mm.then_inc(s["mod_done"], 1)
            for g, col in enumerate((2, 5)):
                for k in range(KD):
                    mm = pe.matmul(bank[0:B, 7, g * D:(g + 1) * D], silu_c[:, k, :], wmod32[:, k, col * D:(col + 1) * D],
                                   start=(k == 0), stop=(k == KD - 1))
            mm.then_inc(s["mod_done"], 1)
            pe.wait_ge(s["ident_ready"], 2)
            pe.wait_ge(s["wsplit_l"], 3)
            pe.wait_ge(s["modv_ready"], 2)
            pe.wait_ge(s["gr_ready"], 1)

            def product(dst, weights, moving, pieces, count=None):
                terms = [pair for k in range(pieces) for pair in passes(*weights(k), *moving(k))]
                for i, (w, a) in enumerate(terms):
                    mm = pe.matmul(dst, w, a, start=(i == 0), stop=(i == len(terms) - 1))
                return mm

            def iteration(c):
                n, o, a = c.at(1), c.at(-1), c.at(-2)

                def gate_up_piece(i):
                    if a.real:
                        e, j = i // IJ, i % IJ
                        wait(pe, s["wgu_l"], i + 1)
                        if i == 0:
                            wait(pe, s["h2h_ready"], a.n + 1)
                            wait(pe, s["h2l_ready"], a.n + 1)
                        wait(pe, s["hfe_ready"], CHUNKS * a.n + i)
                        tokens = bass.ds(S * a.n, S)
                        for g in range(2):
                            mm = product(bank[:, 5, g * S:(g + 1) * S],
                                         lambda k: (gu_h[:, e, j, (g * KD + k) * P:(g * KD + k + 1) * P],
                                                    gu_l[:, e, j, (g * KD + k) * P:(g * KD + k + 1) * P]),
                                         lambda k: (h2h[:, k, tokens], h2l[:, k, tokens]), KD)
                        mm.then_inc(s["gue_done"], 1)

                def early_down(e, t):
                    if a.real:
                        if t == 0:
                            wait(pe, s["wdn_l"], e + 1)
                            wait(pe, s["hidel_ready"], CHUNKS * a.n + IJ * (e + 1))
                            if e > 0 and o.real:
                                wait(pe, s["h2T_ready"], 2 * (o.n + 1))
                            elif c.real:
                                wait(pe, s["nm_ready"], c.n + 1)
                            elif o.real:
                                wait(pe, s["aT_ready"], 2 * (o.n + 1))
                            wait(pe, s["acc_ready"], CLEARED + TT * (EARLY * a.n + e))
                        mm = product(bank[:, 7, t * D:(t + 1) * D],
                                     lambda j: (hid_eh[:, e, j, t * P:(t + 1) * P], hid_el[:, e, j, t * P:(t + 1) * P]),
                                     lambda j: (dn_h[:, e, j, :], dn_l[:, e, j, :]), IJ)
                        mm.then_inc(s["ye_done"], 1)

                def scores(c, pair):
                    if not c.real:
                        return
                    if pair == 0:
                        wait(pe, stack_in[c.par], 12 * 16 * (c.half + 1))
                    if pair < 2:
                        wait(pe, s["exp_done"], PAIRS * c.n - 1 + pair)
                    else:
                        wait(pe, s["max_done"], PAIRS * c.n + pair - 1)
                    for t in range(TT):
                        for odd in range(2):
                            rows = slice(64 * odd, 64 * odd + STACK)
                            mm = pe.matmul(bank[:, 2 * (pair % 2) + odd, t * S:(t + 1) * S],
                                           qst[rows, c.par, pair, t * P:(t + 1) * P], kst[rows, c.par, pair, :],
                                           start=True, stop=True)
                    mm.then_inc(s["sc_done"], 1)

                def scores_transposed(pair):
                    if not c.real:
                        return
                    if pair == 0:
                        wait(pe, nm_in[c.par], 32 * (c.half + 1))
                    if pair < 2:
                        wait(pe, s["max_done"], PAIRS * c.n + PAIRS - 1 + pair)
                    else:
                        wait(pe, s["exp_done"], PAIRS * c.n + pair - 1)
                    for t in range(TT):
                        for odd in range(2):
                            rows = slice(64 * odd, 64 * odd + STACK + 1)
                            mm = pe.matmul(bank[:, 2 * (pair % 2) + odd, t * S:(t + 1) * S],
                                           kst[rows, c.par, pair, t * P:(t + 1) * P], qst[rows, c.par, pair, :],
                                           start=True, stop=True)
                    mm.then_inc(s["scT_done"], 1)

                def weighted_values(pair):
                    if not c.real:
                        return
                    group = pair // 2
                    wait(pe, s["exp_done"], PAIRS * c.n + pair + 1)
                    if pair == 0:
                        wait(pe, s["v_ready"], TT * (c.n + 1))
                    if pair % 4 == 0:
                        wait(pe, s["au_ready"], 2 * c.n + pair // 4)
                    for t in range(TT):
                        for odd in range(2):
                            col = 2 * (pair % 2) + odd
                            mm = pe.matmul(bank[VW * col:VW * (col + 1), 4, (group % 2) * S:(group % 2 + 1) * S],
                                           vx[:, c.par, t, 2 * pair + odd, :], prob[:, pair % 2, odd, t, :],
                                           start=(t == 0), stop=(t == TT - 1), skip_group_check=True,
                                           tile_position=(0, VW * col))
                    mm.then_inc(s["pv_done"], 1)

                def transpose_tiles(which, src, done):
                    for k in range(KD):
                        for t in range(TT):
                            mm = pe.transpose(bank[:, which, k * S + t * P:k * S + (t + 1) * P], src[:, t, k * P:(k + 1) * P], ident[:, :])
                    mm.then_inc(s[done], 1)

                def ln1_transposed():
                    if n.real:
                        if isinstance(c.n, int) and c.n < 2:
                            wait(pe, s["v_ready"], TT * n.n)
                        wait(pe, s["lsh_ready"], c.n - 1)
                        wait(pe, s["xn1_ready"], TT * (n.n + 1))
                        transpose_tiles(6, xn1, "t1_done")

                def attention_by_token(t):
                    if o.real:
                        if t == 0:
                            wait(pe, s["au_ready"], 2 * (o.n + 1))
                            wait(pe, s["h2T_ready"], 2 * o.n)
                            if c.at(-3).real:
                                wait(pe, s["acc_ready"], CLEARED + TT * EARLY * (c.n - 2))
                        elif n.real:
                            wait(pe, s["hT_ready"], 2 * (n.n + 1))
                        else:
                            wait(pe, s["lsh_ready"], o.n)
                        for g in range(4):
                            mm = pe.transpose(bank[:, 7 - t, g * P:(g + 1) * P], au[:, g, t * P:(t + 1) * P], ident[:, :])
                        mm.then_inc(s["tn_done"], 1)

                def q_or_k(which):
                    if n.real:
                        done, piece = (("qp_done", 0), ("kp_done", 2))[which]
                        wait(pe, s["hh_ready"], n.n + 1)
                        wait(pe, s["hl_ready"], n.n + 1)
                        if o.real:
                            wait(pe, s["at_ready"], TT * o.n + which + 1)
                        elif which == 0:
                            wait(pe, s["q32_ready"], 2 * n.n)
                        else:
                            wait(pe, s["hT_ready"], 2 * (n.n + 1))
                        for m in range(2):
                            cols = slice((piece + m) * P, (piece + m + 1) * P)
                            mm = product(bank[:, 7 - which, m * S:(m + 1) * S],
                                         lambda k: (wq_h[:, k, cols], wq_l[:, k, cols]),
                                         lambda k: (hh[:, k, :], hl[:, k, :]), KD)
                        mm.then_inc(s[done], 1)

                def attention_transposed():
                    if o.real:
                        wait(pe, s["at_ready"], TT * (o.n + 1))
                        if n.real:
                            wait(pe, s["q32_ready"], 2 * (n.n + 1))
                        transpose_tiles(7, at, "ta_done")

                def v():
                    if n.real:
                        wait(pe, s["k32_ready"], 2 * (n.n + 1))
                        for t in range(TT):
                            mm = product(bank[:, 6, t * D:(t + 1) * D],
                                         lambda k: (hh[:, k, t * P:(t + 1) * P], hl[:, k, t * P:(t + 1) * P]),
                                         lambda k: (wq_h[:, k, 2 * D:3 * D], wq_l[:, k, 2 * D:3 * D]), KD)
                        mm.then_inc(s["vp_done"], 1)

                def maxima_transposed():
                    if c.real:
                        wait(pe, s["max_done"], PAIRS * (c.n + 1))
                        if o.real:
                            wait(pe, s["aT_ready"], 2 * (o.n + 1))
                        elif n.real:
                            wait(pe, s["q32_ready"], 2 * (n.n + 1))
                        for t in range(TT):
                            mm = pe.transpose(bank[0:H, 7, t * P:(t + 1) * P],
                                              mx[:, t, :, :].rearrange("p o s -> p (o s)"), ident[:, :])
                        mm.then_inc(s["nmt_done"], 1)

                def output_projection():
                    if o.real:
                        wait(pe, s["ah_ready"], o.n + 1)
                        wait(pe, s["al_ready"], o.n + 1)
                        if n.real:
                            wait(pe, s["v_ready"], TT * (n.n + 1))
                        for t in range(TT):
                            mm = product(bank[:, 6, t * D:(t + 1) * D],
                                         lambda k: (ah[:, k, t * P:(t + 1) * P], al[:, k, t * P:(t + 1) * P]),
                                         lambda k: (wo_h[:, k, :], wo_l[:, k, :]), KD)
                        mm.then_inc(s["op_done"], 1)

                def ln2_transposed():
                    if o.real:
                        wait(pe, s["xn2_ready"], TT * (o.n + 1))
                        if c.real:
                            wait(pe, s["nm_ready"], c.n + 1)
                        if a.real:
                            wait(pe, s["acc_ready"], CLEARED + TT * (EARLY * a.n + 1))
                        transpose_tiles(7, xn2, "t2_done")

                def router():
                    if o.real:
                        wait(pe, s["h2h_ready"], o.n + 1)
                        wait(pe, s["h2l_ready"], o.n + 1)
                        for t in range(TT):
                            tokens = bass.ds(S * o.n + t * P, P)
                            mm = product(bank[:, 6, t * E:(t + 1) * E],
                                         lambda k: (h2h[:, k, tokens], h2l[:, k, tokens]),
                                         lambda k: (wr_h[:, k, :], wr_l[:, k, :]), KD)
                        mm.then_inc(s["rt_done"], 1)

                gate_up_piece(0)
                ln1_transposed()
                scores(c, 2)
                attention_by_token(0)
                scores(c, 3)
                attention_by_token(1)
                gate_up_piece(1)
                q_or_k(0)
                scores(c, 4)
                gate_up_piece(2)
                q_or_k(1)
                attention_transposed()
                scores(c, 5)
                gate_up_piece(3)
                v()
                scores(c, 6)
                gate_up_piece(4)
                scores(c, 7)
                output_projection()
                maxima_transposed()
                gate_up_piece(5)
                early_down(0, 0)
                early_down(0, 1)
                scores_transposed(0)
                scores_transposed(1)
                gate_up_piece(6)
                weighted_values(0)
                scores_transposed(2)
                weighted_values(1)
                scores_transposed(3)
                weighted_values(2)
                gate_up_piece(7)
                scores_transposed(4)
                weighted_values(3)
                scores_transposed(5)
                weighted_values(4)
                ln2_transposed()
                scores_transposed(6)
                weighted_values(5)
                scores_transposed(7)
                early_down(1, 0)
                weighted_values(6)
                scores(n, 0)
                weighted_values(7)
                scores(n, 1)
                early_down(1, 1)
                router()

            run_stage_one(pe, iteration)

            def gate_up(e, blk, j, first):
                done = IJ * (NB * e + blk)
                if first:
                    wait(pe, s["wgu_l"], IJ * (EARLY + e) + j + 1)
                wait(pe, s["hf_ready"], done + j - 1)
                tokens = bass.ds(TB * blk, TB)
                for g in range(2):
                    mm = product(bank[:, 2 * (j % 2) + g, :],
                                 lambda k: (gu_h[:, 0, j, (g * KD + k) * P:(g * KD + k + 1) * P],
                                            gu_l[:, 0, j, (g * KD + k) * P:(g * KD + k + 1) * P]),
                                 lambda k: (h2h[:, k, tokens], h2l[:, k, tokens]), KD)
                mm.then_inc(s["gu_done"], 1)

            def down(e, blk, par, t):
                done = BT * (NB * e + blk)
                if t == 0:
                    wait(pe, s["wdn_l"], EARLY + e + 1)
                    wait(pe, s["hidl_ready"], IJ * (NB * e + blk + 1))
                wait(pe, s["acc_ready"], CLEARED + NT * EARLY + done + t + 1 - BT)
                mm = product(bank[:, 4 + t, 0:D],
                             lambda j: (hid_h[:, par, j, t * P:(t + 1) * P], hid_l[:, par, j, t * P:(t + 1) * P]),
                             lambda j: (dn_h[:, 0, j, :], dn_l[:, 0, j, :]), IJ)
                mm.then_inc(s["y_done"], 1)

            def step(e, blk, par, before, refill_gu=False, refill_dn=False):
                for j in range(IJ):
                    gate_up(e, blk, j, first=(before is None or refill_dn))
                    if before is not None:
                        down(*before, 1 - par, j)

            def drain(e, blk, par):
                for t in range(BT):
                    down(e, blk, par, t)

            pe.wait_ge(s["lsh_ready"], B)
            pe.wait_ge(s["au_ready"], 2 * B)
            pe.wait_ge(s["hfe_ready"], CHUNKS * B)
            pe.wait_ge(s["acc_ready"], CLEARED + NT * EARLY)
            run_stage_two(pe, step, drain)


def kernel(**inputs):
    import numpy as np
    import concourse.bacc as bacc
    from concourse.bass_utils import run_bass_kernel_spmd

    t = lambda name: np.asarray(inputs[name])
    arrays = {
        "x": t("L0_attn_x"),
        "wqkv_t": t("L0_attn_w_qkv").T,
        "bqkv_p": t("L0_attn_b_qkv").reshape(6, P).T,
        "wo_t": t("L0_attn_w_o").T,
        "b_o": t("L0_attn_b_o"),
        "router_t": t("L0_ffn_router_w").T,
        "gate_t": t("L0_ffn_gate_w").transpose(0, 2, 1),
        "up_t": t("L0_ffn_up_w").transpose(0, 2, 1),
        "down_t": t("L0_ffn_down_w").transpose(0, 2, 1),
        "c_t": t("L0_c").T,
        "wmod": t("L0_wmod"),
    }
    arrays = {f"in_{k}": np.ascontiguousarray(v) for k, v in arrays.items()}
    nc = bacc.Bacc("TRN2", target_bir_lowering=False, num_devices=1)
    args = [nc.dram_tensor(k, v.shape, mybir.dt.from_np(v.dtype), kind="ExternalInput").ap() for k, v in arrays.items()]
    out = nc.dram_tensor("out", (B, S, D), F32, kind="ExternalOutput").ap()
    adaln_block(nc, *args, out)
    r = run_bass_kernel_spmd(nc, [arrays], core_ids=[0])
    return r.results[0]["out"]
```

```python
from contextlib import ExitStack

import concourse.bass as bass
from concourse import mybir

F32 = mybir.dt.float32
F16 = mybir.dt.float16
ALU = mybir.AluOpType
ACT = mybir.ActivationFunctionType
AX = mybir.AxisListType

P = 128
B, S, D = 16, 256, 256
H, HD = 16, 16
E, I = 8, 512
KD = D // P
TT = S // P
NT = B * TT
PAIRS = H // 2
GROUPS = H // 4
EPS = 1e-5
TOP_P = 0.9
GATE_MIN = 0.25

XS = 16.0
WS = 256.0
QS = XS / HD ** 0.5
SS = XS * XS
MAXK = 256.0
VW = 32
STACK = 3 * HD

EARLY = 2
LATE = E - EARLY
TB = 512
NB = B * S // TB
BT = TB // P
IJ = I // P
CHUNKS = EARLY * IJ
CLEARED = 4
GU_SCALE = XS * WS
WPIECE = 2 * KD * P
STAGED = 2 * KD * I + IJ * D


class Batch:

    def __init__(self, half, par):
        self.half, self.par = half, par
        self.n = 2 * half + par

    def at(self, d):
        p = self.par + d
        return Batch(self.half + p // 2, p % 2)

    @property
    def real(self):
        return not isinstance(self.n, int) or 0 <= self.n < B


def wait(engine, sem, value):
    if isinstance(value, int) and value <= 0:
        return
    engine.wait_ge(sem, value)


def adaln_block(nc, x, wqkv_t, bqkv_p, wo_t, b_o, router_t, gate_t, up_t, down_t, c_t, wmod, out):
    with ExitStack() as ctx:
        def sb(name, shape, dt=F32):
            return ctx.enter_context(nc.sbuf_tensor(name, shape, dt))

        def sem(name):
            return ctx.enter_context(nc.semaphore(name))

        bank = ctx.enter_context(nc.psum_tensor("bank", [P, 8, 512], F32))

        acc = sb("acc", [P, NT, D])
        h2h = sb("h2h", [P, KD, B * S], F16)
        h2l = sb("h2l", [P, KD, B * S], F16)
        wts = sb("wts", [P, NT, E])
        ident = sb("ident", [P, P])

        wq_h = sb("wq_h", [P, KD, 3 * D], F16)
        wq_l = sb("wq_l", [P, KD, 3 * D], F16)
        wo_h = sb("wo_h", [P, KD, D], F16)
        wo_l = sb("wo_l", [P, KD, D], F16)
        wr_h = sb("wr_h", [P, KD, E], F16)
        wr_l = sb("wr_l", [P, KD, E], F16)
        bias_p = sb("bias_p", [P, 6])
        bias_s = sb("bias_s", [P, 6])
        bo_bc = sb("bo_bc", [P, D])
        silu_c = sb("silu_c", [P, KD, B])
        tanh_c = sb("tanh_c", [P, KD, B])
        modv = sb("modv", [P, 4, KD, B])
        gate_r = sb("gate_r", [B, 2, D])
        earlier = sb("earlier", [P, E, E])
        halfpow = sb("halfpow", [P, TT])
        eps = sb("eps", [P, TT])

        xa = sb("xa", [P, 2, TT, D])
        xr = sb("xr", [P, 2, TT, D])
        qst = sb("qst", [P, 2, PAIRS, S], F16)
        kst = sb("kst", [P, 2, PAIRS, S], F16)
        vx = sb("vx", [P, 2, TT, H, VW])
        prob = sb("prob", [P, 2, 4, TT, S])
        bn1 = sb("bn1", [P, TT, 6])
        parts1 = sb("parts1", [P, TT, 4])
        mv1 = sb("mv1", [P, TT, 2])
        ve1 = sb("ve1", [P, TT])
        rs1 = sb("rs1", [P, TT])
        xn1 = sb("xn1", [P, TT, D])
        bn2 = sb("bn2", [P, TT, 6])
        parts2 = sb("parts2", [P, TT, 4])
        mv2 = sb("mv2", [P, TT, 2])
        ve2 = sb("ve2", [P, TT])
        rs2 = sb("rs2", [P, TT])
        xn2 = sb("xn2", [P, TT, D])
        hT = sb("hT", [P, KD, S])
        hh = sb("hh", [P, KD, S], F16)
        hl = sb("hl", [P, KD, S], F16)
        q32 = sb("q32", [P, KD, S])
        qh = sb("qh", [P, KD, S], F16)
        ql = sb("ql", [P, KD, S], F16)
        k32 = sb("k32", [P, KD, S])
        kh = sb("kh", [P, KD, S], F16)
        kl = sb("kl", [P, KD, S], F16)
        mx = sb("mx", [P, TT, 2, PAIRS])
        nm = sb("nm", [H, S], F16)
        au = sb("au", [P, 4, S])
        rec = sb("rec", [P, TT, H])
        at = sb("at", [P, TT, D])
        aT = sb("aT", [P, KD, S])
        ah = sb("ah", [P, KD, S], F16)
        al = sb("al", [P, KD, S], F16)
        ga_bc = sb("ga_bc", [P, D])
        proj = sb("proj", [P, TT, D])
        h2T = sb("h2T", [P, KD, S])
        lmax = sb("lmax", [P, TT])
        lsh = sb("lsh", [P, TT, E])
        pexp = sb("pexp", [P, TT, E])
        psum_r = sb("psum_r", [P, TT])
        prec = sb("prec", [P, TT])
        rp = sb("rp", [P, TT, E])
        before = sb("before", [P, TT, E, E])
        ties = sb("ties", [P, TT, E, E])
        cum = sb("cum", [P, TT, E])

        gate_s, gate_m = xn2[0:B, :, :], h2T[0:B, :, :]
        th_e = sb("th_e", [P, S])
        sg_e = sb("sg_e", [P, S])
        hf_e = sb("hf_e", [P, 2, S])
        hid_eh = sb("hid_eh", [P, EARLY, IJ, S], F16)
        hid_el = sb("hid_el", [P, EARLY, IJ, S], F16)

        staged = sb("staged", [P, STAGED])
        gu_h = sb("gu_h", [P, EARLY, IJ, WPIECE], F16)
        gu_l = sb("gu_l", [P, EARLY, IJ, WPIECE], F16)
        dn_h = sb("dn_h", [P, EARLY, IJ, D], F16)
        dn_l = sb("dn_l", [P, EARLY, IJ, D], F16)
        hid_h = qst[:, :, :, :].rearrange("p a b c -> p (a b c)").rearrange("p (h j n) -> p h j n", h=2, j=IJ)
        hid_l = kst[:, :, :, :].rearrange("p a b c -> p (a b c)").rearrange("p (h j n) -> p h j n", h=2, j=IJ)
        probv = prob[:, :, :, :, :].rearrange("p a b c d -> p (a b c d)")
        th = [probv[:, 0:TB], probv[:, TB:2 * TB]]
        sg = [probv[:, 2 * TB:3 * TB], probv[:, 3 * TB:4 * TB]]
        hf = [hT[:, :, :].rearrange("p k s -> p (k s)"), q32[:, :, :].rearrange("p k s -> p (k s)")]
        gb_bc = at
        x1l = au[:, :, :]
        gbl = proj[:, :, :]
        x1f = vx[:, :, :, :, :].rearrange("p a b c d -> p (a b c d)")[:, 0:BT * D].rearrange("p (t d) -> p t d", t=BT)
        fin = vx[:, :, :, :, :].rearrange("p a b c d -> p (a b c d)")[:, BT * D:2 * BT * D].rearrange("p (t d) -> p t d", t=BT)

        accf = acc[:, :, :].rearrange("p t d -> p (t d)")
        o_mod, o_qkv = 0, KD * 6 * D
        o_wo = o_qkv + KD * 3 * D
        o_r = o_wo + KD * D
        o_c = o_r + KD * E
        wmod32 = accf[:, o_mod:o_qkv].rearrange("p (k n) -> p k n", k=KD)
        wq32 = accf[:, o_qkv:o_wo].rearrange("p (k n) -> p k n", k=KD)
        wo32 = accf[:, o_wo:o_r].rearrange("p (k n) -> p k n", k=KD)
        wr32 = accf[:, o_r:o_c].rearrange("p (k n) -> p k n", k=KD)
        c32 = accf[:, o_c:o_c + KD * B].rearrange("p (k n) -> p k n", k=KD)
        staged_gu = staged[:, 0:2 * KD * I].rearrange("p (g n) -> p g n", g=2 * KD)
        staged_dn = staged[:, 2 * KD * I:STAGED]

        q_d = nc.dram_tensor("q_scratch", [2, 2, D, S], F16, kind="Internal").ap()
        k_d = nc.dram_tensor("k_scratch", [2, 2, D, S], F16, kind="Internal").ap()
        x1_d = nc.dram_tensor("residual", [B, S, D], F32, kind="Internal").ap()
        gates_d = nc.dram_tensor("gates_scratch", [2, B, D], F32, kind="Internal").ap()

        names = """c_in wmod_in wmod_rest_in wqkv_in wo_in bias_in bo_in bias_s_ready ident_ready tanhc_ready siluc_ready mod_done
            modv_ready gr_ready gates_ready gates_out wsplit_h wsplit_l consts_ready pow_ready
            ga_in scr_written st1_ready halves1_ready parts1_ready mv1_ready ve1_ready rs1_ready xn1_ready t1_done hT_ready hh_ready hl_ready
            qp_done q32_ready qh_ready ql_ready kp_done k32_ready kh_ready kl_ready vp_done v_ready
            sc_done max_done nmt_done nm_ready scT_done exp_done pv_done au_ready tn_done rec_ready at_ready
            ta_done aT_ready ah_ready al_ready op_done proj_ready gated_ready x1_ready
            st2_ready halves2_ready parts2_ready mv2_ready ve2_ready rs2_ready xn2_ready t2_done h2T_ready h2h_ready h2l_ready
            rt_done lmax_ready lsh_ready pexp_ready rsum_ready prec_ready rp_ready before_ready ties_ready
            tied_ready joined_ready weighed_ready cum_ready w_ready
            gu_in dn_in wgu_h wgu_l wdn_h wdn_l gu_done th_ready sg_ready hf_ready hidh_ready hidl_ready
            y_done acc_ready gb_in fin_mul fin_add out_done
            gue_done the_ready sge_ready hfe_ready hideh_ready hidel_ready ye_done x1f_in last_in last_mul last_add""".split()
        s = {n: sem(n) for n in names}
        x_in = [sem(f"x_in{p}") for p in range(2)]
        stack_in = [sem(f"stack_in{p}") for p in range(2)]
        xr_in = [sem(f"xr_in{p}") for p in range(2)]
        x1_out = [sem(f"x1_out{p}") for p in range(2)]
        nm_in = [sem(f"nm_in{p}") for p in range(2)]

        def passes(w_hi, w_lo, a_hi, a_lo):
            return ((w_hi, a_hi), (w_hi, a_lo), (w_lo, a_hi))

        def early_bank(c, i):
            return 5 if c.real or i % 2 == 0 else 0

        def down_bank(c, e):
            return 7 if c.real else (4, 5)[e]

        def run_stage_one(engine, iteration, between={}):
            for n in range(-3, 4):
                if n in between:
                    between[n]()
                iteration(Batch(n // 2, n % 2))
            with engine.Fori(2, (B - 2) // 2) as half:
                iteration(Batch(half, 0))
                iteration(Batch(half, 1))
            for n in range(B - 2, B + 2):
                if n in between:
                    between[n]()
                iteration(Batch(n // 2, n % 2))

        def run_stage_two(engine, step, drain):
            def middle(e):
                with engine.Fori(0, NB // 2 - 1) as m:
                    step(e, 2 * m + 1, 1, before=(e, 2 * m))
                    step(e, 2 * m + 2, 0, before=(e, 2 * m + 1))

            step(0, 0, 0, before=None)
            with engine.Fori(0, LATE - 1) as e:
                middle(e)
                step(e, NB - 1, 1, before=(e, NB - 2), refill_gu=True)
                step(e + 1, 0, 0, before=(e, NB - 1), refill_dn=True)
            middle(LATE - 1)
            step(LATE - 1, NB - 1, 1, before=(LATE - 1, NB - 2))
            drain(LATE - 1, NB - 1, 1)

        block = ctx.enter_context(nc.Block())

        @block.sync
        def _(sp):
            def load_x(m):
                wait(sp, s["xn1_ready"], TT * (m.n - 1))
                sp.dma_start(xa[:, m.par, :, :],
                             x[bass.ds(m.n, 1)].rearrange("a (t p) d -> p (a t) d", p=P)).then_inc(x_in[m.par], 16)

            sp.dma_start(c32, c_t.rearrange("(k p) b -> p k b", p=P)).then_inc(s["c_in"], 16)
            wmod_rows = wmod.rearrange("(k p) n -> p k n", p=P)
            sp.dma_start(wmod32[:, :, 0:2 * D], wmod_rows[:, :, 0:2 * D]).then_inc(s["wmod_in"], 16)
            load_x(Batch(0, 0))
            sp.dma_start(bias_p[:, :], bqkv_p).then_inc(s["bias_in"], 16)
            sp.dma_start(wq32, wqkv_t.rearrange("(k p) n -> p k n", p=P)).then_inc(s["wqkv_in"], 16)
            sp.dma_start(wmod32[:, :, 2 * D:6 * D], wmod_rows[:, :, 2 * D:6 * D]).then_inc(s["wmod_rest_in"], 16)
            sp.dma_start(wo32, wo_t.rearrange("(k p) n -> p k n", p=P)).then_inc(s["wo_in"], 16)
            sp.dma_start(wr32, router_t.rearrange("(k p) n -> p k n", p=P)).then_inc(s["wo_in"], 16)
            sp.dma_start(bo_bc[:, :], b_o.partition_broadcast(P)).then_inc(s["bo_in"], 16)

            def load_expert(e):
                for g, w in enumerate((gate_t, up_t)):
                    sp.dma_start(staged_gu[:, g * KD:(g + 1) * KD, :],
                                 w[bass.ds(e, 1)].rearrange("a (k p) i -> p (a k) i", p=P)).then_inc(s["gu_in"], 16)
                sp.dma_start(staged_dn.rearrange("p (j d) -> p j d", j=IJ),
                             down_t[bass.ds(e, 1)].rearrange("a (j p) d -> p (a j) d", p=P)).then_inc(s["dn_in"], 16)

            def store_gates():
                wait(sp, s["gates_ready"], 2)
                sp.dma_start(gates_d.rearrange("g b d -> b g d"), gate_r[:, :, :]).then_inc(s["gates_out"], 16)

            def load_first():
                wait(sp, s["consts_ready"], 4)
                load_expert(0)

            def iteration(c):
                n, o, ahead = c.at(1), c.at(-1), c.at(2)
                if ahead.real and not (isinstance(ahead.n, int) and ahead.n == 0):
                    load_x(ahead)
                if n.real:
                    wait(sp, stack_in[n.par], 12 * 16 * n.half)
                    wait(sp, s["qh_ready"], n.n + 1)
                    wait(sp, s["ql_ready"], n.n + 1)
                    for part, src in enumerate((qh, ql)):
                        sp.dma_start(q_d[n.par, part].rearrange("(k p) s -> p k s", p=P), src[:, :, :]).then_inc(s["scr_written"], 16)
                if c.real:
                    wait(sp, x1_out[c.par], 16 * c.half)
                    wait(sp, s["xn2_ready"], TT * c.n - TT)
                    sp.dma_start(xr[:, c.par, :, :],
                                 x[bass.ds(c.n, 1)].rearrange("a (t p) d -> p (a t) d", p=P)).then_inc(xr_in[c.par], 16)
                    wait(sp, s["nm_ready"], c.n + 1)
                    for odd in range(2):
                        sp.dma_start(qst[64 * odd + STACK:64 * odd + STACK + 1, c.par, :, :],
                                     nm[PAIRS * odd:PAIRS * (odd + 1), :]).then_inc(nm_in[c.par], 16)
                if n.real:
                    wait(sp, s["kh_ready"], n.n + 1)
                    wait(sp, s["kl_ready"], n.n + 1)
                    for part, src in enumerate((kh, kl)):
                        sp.dma_start(k_d[n.par, part].rearrange("(k p) s -> p k s", p=P), src[:, :, :]).then_inc(s["scr_written"], 16)
                    wait(sp, s["scr_written"], 64 * (n.n + 1))
                    wait(sp, s["scT_done"], PAIRS * n.n - PAIRS)
                    for odd in range(2):
                        for r, (qpart, kpart) in enumerate(((0, 0), (0, 1), (1, 0))):
                            row = 64 * odd + HD * r
                            for stack, scratch, part in ((qst, q_d, qpart), (kst, k_d, kpart)):
                                src = scratch[n.par, part].rearrange("(s o d) t -> o d s t", o=2, d=HD)[odd]
                                sp.dma_start(stack[row:row + HD, n.par, :, :], src).then_inc(stack_in[n.par], 16)
                if o.real:
                    wait(sp, s["x1_ready"], o.n + 1)
                    sp.dma_start(x1_d[bass.ds(o.n, 1)].rearrange("a (t p) d -> p (a t) d", p=P),
                                 xr[:, o.par, :, :]).then_inc(x1_out[o.par], 16)
                if c.real:
                    if isinstance(c.n, int) and c.n == 0:
                        wait(sp, s["gates_out"], 16)
                    wait(sp, s["gated_ready"], c.n)
                    sp.dma_start(ga_bc[:, :], gates_d[0, bass.ds(c.n, 1), :].rearrange("a d -> (a d)").partition_broadcast(P)).then_inc(s["ga_in"], 16)

            def load_next(e):
                wait(sp, s["wgu_h"], IJ * e)
                wait(sp, s["wgu_l"], IJ * e)
                wait(sp, s["wdn_h"], e)
                wait(sp, s["wdn_l"], e)
                load_expert(e)

            run_stage_one(sp, iteration, {-1: load_first, 0: store_gates, 1: lambda: load_next(1), B - 2: lambda: load_next(2)})

            with sp.Fori(EARLY + 1, E) as e:
                load_next(e)
            for p in range(2):
                wait(sp, x1_out[p], 16 * B // 2)

            def finish(blk):
                sp.dma_start(gb_bc[:, :, :].rearrange("p b d -> p (b d)"),
                             gates_d[1, bass.ds(2 * blk, 2), :].rearrange("b d -> (b d)").partition_broadcast(P)).then_inc(s["gb_in"], 16)
                sp.dma_start(x1f, x1_d[bass.ds(2 * blk, 2)].rearrange("b (t p) d -> p (b t) d", p=P)).then_inc(s["x1f_in"], 16)
                wait(sp, s["fin_add"], blk + 1)
                sp.dma_start(out[bass.ds(2 * blk, 2)].rearrange("b (t p) d -> p (b t) d", p=P),
                             fin).then_inc(s["out_done"], 16)

            last = NB - 1
            sp.dma_start(gbl.rearrange("p b d -> p (b d)"),
                         gates_d[1, 2 * last:2 * NB, :].rearrange("b d -> (b d)").partition_broadcast(P)).then_inc(s["last_in"], 16)
            sp.dma_start(x1l, x1_d[2 * last:2 * NB].rearrange("b (t p) d -> p (b t) d", p=P)).then_inc(s["last_in"], 16)
            with sp.Fori(0, last) as blk:
                finish(blk)
            for b in range(2):
                wait(sp, s["last_add"], TT * (b + 1))
                sp.dma_start(out[2 * last + b].rearrange("(t p) d -> p t d", p=P),
                             acc[:, NT - BT + TT * b:NT - BT + TT * (b + 1), :]).then_inc(s["out_done"], 16)
            wait(sp, s["out_done"], 16 * (NB + 1))

        @block.gpsimd
        def _(pool):
            pool.memset(ident[:, :], 0.0).then_inc(s["ident_ready"], 1)
            pool.wait_ge(s["ident_ready"], 1)
            pool.affine_select(out=ident[:, :], in_=ident[:, :], compare_op=ALU.not_equal, fill=1.0, base=0,
                               pattern=[[-1, P]], channel_multiplier=1).then_inc(s["ident_ready"], 1)
            pool.memset(halfpow[:, :], -0.5).then_inc(s["pow_ready"], 1)
            pool.memset(eps[:, :], EPS).then_inc(s["pow_ready"], 1)
            pool.wait_ge(s["pow_ready"], 2)
            pool.memset(earlier[:, :, :], 1.0).then_inc(s["consts_ready"], 1)
            pool.wait_ge(s["consts_ready"], 1)
            pool.affine_select(out=earlier[:, :, :], in_=earlier[:, :, :], compare_op=ALU.is_gt, fill=0.0, base=0,
                               pattern=[[1, E], [-1, E]], channel_multiplier=0).then_inc(s["consts_ready"], 1)
            pool.memset(kst[:, :, :, :].rearrange("p a b c -> p (a b c)"), MAXK).then_inc(s["consts_ready"], 1)
            pool.memset(vx[:, :, :, :, :].rearrange("p a b c d -> p (a b c d)"), 1.0).then_inc(s["consts_ready"], 1)

            def clear_acc():
                pool.wait_ge(s["mod_done"], 3)
                pool.wait_ge(s["siluc_ready"], 1)
                pool.wait_ge(s["wsplit_h"], 3)
                pool.wait_ge(s["wsplit_l"], 3)
                for q in range(CLEARED):
                    pool.memset(acc[:, q * NT // CLEARED:(q + 1) * NT // CLEARED, :].rearrange("p t d -> p (t d)"), 0.0).then_inc(s["acc_ready"], 1)

            def inverse_deviation(mv, ve, rs, mv_sem, ve_sem, rs_sem, n):
                pool.wait_ge(s[mv_sem], TT * (n + 1))
                pool.tensor_tensor(ve[:, :], mv[:, :, 1], eps[:, :], ALU.add).then_inc(s[ve_sem], 1)
                pool.wait_ge(s[ve_sem], n + 1)
                pool.tensor_tensor(rs[:, :], ve[:, :], halfpow[:, :], ALU.pow).then_inc(s[rs_sem], 1)

            def hidden_low(a, i):
                if a.real:
                    wait(pool, s["hideh_ready"], CHUNKS * a.n + i + 1)
                    pool.tensor_tensor(hid_el[:, i // IJ, i % IJ, :], hf_e[:, i % 2, :], hid_eh[:, i // IJ, i % IJ, :],
                                       ALU.subtract).then_inc(s["hidel_ready"], 1)

            def iteration(c):
                n, o, a, m = c.at(1), c.at(-1), c.at(-2), c.at(2)
                if n.real:
                    wait(pool, s["hh_ready"], n.n + 1)
                    wait(pool, s["vp_done"], n.n)
                    pool.tensor_tensor(hl[:, :, :], hT[:, :, :], hh[:, :, :], ALU.subtract).then_inc(s["hl_ready"], 1)
                hidden_low(a, 0)
                hidden_low(a, 1)
                if n.real:
                    wait(pool, s["qh_ready"], n.n + 1)
                    pool.tensor_tensor(ql[:, :, :], q32[:, :, :], qh[:, :, :], ALU.subtract).then_inc(s["ql_ready"], 1)
                    wait(pool, s["kh_ready"], n.n + 1)
                    wait(pool, s["scr_written"], 64 * n.n)
                    pool.tensor_tensor(kl[:, :, :], k32[:, :, :], kh[:, :, :], ALU.subtract).then_inc(s["kl_ready"], 1)
                hidden_low(a, 2)
                if o.real:
                    wait(pool, s["ah_ready"], o.n + 1)
                    pool.tensor_tensor(al[:, :, :], aT[:, :, :], ah[:, :, :], ALU.subtract).then_inc(s["al_ready"], 1)
                hidden_low(a, 3)
                hidden_low(a, 4)
                if o.real:
                    wait(pool, s["proj_ready"], o.n + 1)
                    wait(pool, s["ga_in"], 16 * (o.n + 1))
                    pool.tensor_tensor(proj[:, :, :], proj[:, :, :], ga_bc[:, :].unsqueeze(1).to_broadcast([P, TT, D]),
                                       ALU.mult).then_inc(s["gated_ready"], 1)
                    wait(pool, s["gated_ready"], o.n + 1)
                    wait(pool, xr_in[o.par], 16 * (o.half + 1))
                    tile = xr[:, o.par, :, :]
                    pool.tensor_tensor(tile, tile, proj[:, :, :], ALU.add).then_inc(s["x1_ready"], 1)
                hidden_low(a, 5)
                if o.real:
                    inverse_deviation(mv2, ve2, rs2, "mv2_ready", "ve2_ready", "rs2_ready", o.n)
                hidden_low(a, 6)
                if m.real:
                    inverse_deviation(mv1, ve1, rs1, "mv1_ready", "ve1_ready", "rs1_ready", m.n)
                hidden_low(a, 7)

            run_stage_one(pool, iteration, {0: clear_acc})

            def finish(blk):
                pool.wait_ge(s["acc_ready"], CLEARED + BT * (NB * (E - 1) + blk + 1))
                pool.wait_ge(s["gb_in"], 16 * (blk + 1))
                wait(pool, s["out_done"], 16 * blk)
                for b in range(2):
                    pool.tensor_tensor(fin[:, TT * b:TT * (b + 1), :], acc[:, bass.ds(BT * blk + TT * b, TT), :],
                                       gb_bc[:, b, :].unsqueeze(1).to_broadcast([P, TT, D]), ALU.mult).then_inc(s["fin_mul"], 1)
                pool.wait_ge(s["x1f_in"], 16 * (blk + 1))
                pool.wait_ge(s["fin_mul"], 2 * (blk + 1))
                pool.tensor_tensor(fin, fin, x1f, ALU.add).then_inc(s["fin_add"], 1)

            finish(0)
            with pool.Fori(1, NB - 1) as blk:
                finish(blk)

        @block.scalar
        def _(act):
            act.wait_ge(s["c_in"], 16)
            act.activation(tanh_c[:, :, :], c32, ACT.Tanh, scale=0.5).then_inc(s["tanhc_ready"], 1)
            act.wait_ge(s["wqkv_in"], 16)
            act.activation(wq_h[:, :, :], wq32, ACT.Copy, scale=WS).then_inc(s["wsplit_h"], 1)

            def modulated(dst, src, norm, n, done):
                for k in range(KD):
                    act.activation(dst[:, k, :], src[:, k, :], ACT.Identity, scale=modv[:, 2 * norm + 1, k, bass.ds(n, 1)],
                                   bias=modv[:, 2 * norm, k, bass.ds(n, 1)]).then_inc(s[done], 1)

            def split_gu(place, j):
                act.activation(gu_h[:, place, j, :].rearrange("p (g m) -> p g m", g=2 * KD), staged_gu[:, :, j * P:(j + 1) * P],
                               ACT.Copy, scale=WS).then_inc(s["wgu_h"], 1)

            def split_dn(place, e):
                act.wait_ge(s["dn_in"], 16 * (e + 1))
                act.activation(dn_h[:, place, :, :].rearrange("p j d -> p (j d)"), staged_dn, ACT.Copy, scale=WS).then_inc(s["wdn_h"], 1)

            def first_late(j):
                if j == 0:
                    act.wait_ge(s["gu_in"], 32 * (EARLY + 1))
                    act.wait_ge(s["gue_done"], CHUNKS * (B - 1) + IJ)
                split_gu(0, j)

            def tanh_piece(c, a, i):
                if a.real:
                    wait(act, s["gue_done"], CHUNKS * a.n + i + 1)
                    wait(act, s["sge_ready"], CHUNKS * a.n + i)
                    act.activation(th_e[:, :], bank[:, early_bank(c, i), 0:S], ACT.Tanh, scale=0.5 / GU_SCALE).then_inc(s["the_ready"], 1)

            def hidden_high(a, i):
                if a.real:
                    wait(act, s["hfe_ready"], CHUNKS * a.n + i + 1)
                    wait(act, s["ye_done"], TT * EARLY * a.n)
                    act.activation(hid_eh[:, i // IJ, i % IJ, :], hf_e[:, i % 2, :], ACT.Copy).then_inc(s["hideh_ready"], 1)

            def iteration(c):
                n, o, a = c.at(1), c.at(-1), c.at(-2)
                misc = [bank[:, 6 + i, :].rearrange("p (k s) -> p k s", k=2) for i in range(2)]

                def exponentials(pair):
                    if c.real:
                        wait(act, s["scT_done"], PAIRS * c.n + pair + 1)
                        if pair % 2 == 0:
                            wait(act, s["pv_done"], GROUPS * c.n + pair // 2 - 1)
                        r = 2 * (pair % 2)
                        act.activation(prob[:, pair // 2 % 2, r:r + 2, :, :].rearrange("p a b c -> p (a b c)"),
                                       bank[:, r:r + 2, :].rearrange("p a b -> p (a b)"),
                                       ACT.Exp, scale=1.0 / SS).then_inc(s["exp_done"], 1)

                def sums(half):
                    if c.real:
                        wait(act, s["pv_done"], GROUPS * c.n + 2 * (half + 1))
                        wait(act, s["tn_done"], TT * c.n)
                        act.activation(au[:, 2 * half:2 * half + 2, :].rearrange("p g s -> p (g s)"), bank[:, 4, :],
                                       ACT.Copy).then_inc(s["au_ready"], 1)

                if isinstance(c.n, int) and c.n == B + 1:
                    tanh_piece(c, a, 0)
                    for i in range(1, CHUNKS):
                        tanh_piece(c, a, i)
                        hidden_high(a, i - 1)
                        if i > IJ - 1:
                            first_late(i - IJ)
                    hidden_high(a, CHUNKS - 1)
                    act.wait_ge(s["ye_done"], TT * (EARLY * (B - 1) + 1))
                    split_dn(0, EARLY)
                    return

                tanh_piece(c, a, 0)
                if n.real:
                    if isinstance(n.n, int) and n.n == 0:
                        act.wait_ge(s["modv_ready"], 2)
                        act.wait_ge(s["bias_s_ready"], 3)
                    wait(act, s["t1_done"], n.n + 1)
                    wait(act, s["hl_ready"], n.n)
                    modulated(hT, misc[0], 0, n.n, "hT_ready")
                    wait(act, s["hT_ready"], 2 * (n.n + 1))
                    wait(act, s["vp_done"], n.n)
                    act.activation(hh[:, :, :], hT[:, :, :], ACT.Copy).then_inc(s["hh_ready"], 1)
                hidden_high(a, 0)
                tanh_piece(c, a, 1)
                hidden_high(a, 1)
                if n.real:
                    wait(act, s["qp_done"], n.n + 1)
                    wait(act, s["ql_ready"], n.n)
                    for m in range(2):
                        act.activation(q32[:, m, :], misc[1][:, m, :], ACT.Identity, scale=QS / GU_SCALE,
                                       bias=bias_s[:, m:m + 1]).then_inc(s["q32_ready"], 1)
                    wait(act, s["q32_ready"], 2 * (n.n + 1))
                    wait(act, s["scr_written"], 64 * n.n)
                    act.activation(qh[:, :, :], q32[:, :, :], ACT.Copy).then_inc(s["qh_ready"], 1)
                tanh_piece(c, a, 2)
                if n.real:
                    wait(act, s["kp_done"], n.n + 1)
                    wait(act, s["kl_ready"], n.n)
                    for m in range(2):
                        act.activation(k32[:, m, :], misc[0][:, m, :], ACT.Identity, scale=XS / GU_SCALE,
                                       bias=bias_s[:, 2 + m:3 + m]).then_inc(s["k32_ready"], 1)
                    wait(act, s["k32_ready"], 2 * (n.n + 1))
                    act.activation(kh[:, :, :], k32[:, :, :], ACT.Copy).then_inc(s["kh_ready"], 1)
                hidden_high(a, 2)
                tanh_piece(c, a, 3)
                if o.real:
                    wait(act, s["ta_done"], o.n + 1)
                    wait(act, s["al_ready"], o.n)
                    for k in range(KD):
                        act.activation(aT[:, k, :], misc[1][:, k, :], ACT.Identity, scale=XS,
                                       bias=bias_s[:, 4 + k:5 + k]).then_inc(s["aT_ready"], 1)
                    wait(act, s["aT_ready"], 2 * (o.n + 1))
                    wait(act, s["op_done"], o.n)
                    act.activation(ah[:, :, :], aT[:, :, :], ACT.Copy).then_inc(s["ah_ready"], 1)
                if n.real:
                    wait(act, s["vp_done"], n.n + 1)
                    wait(act, s["pv_done"], GROUPS * (n.n - 1))
                    if isinstance(n.n, int) and n.n < 2:
                        act.wait_ge(s["consts_ready"], 4)
                    for t in range(TT):
                        act.activation(vx[:, n.par, t, :, 0:HD], misc[0][:, t, :].rearrange("p (h d) -> p h d", h=H),
                                       ACT.Copy, scale=1.0 / GU_SCALE).then_inc(s["v_ready"], 1)
                hidden_high(a, 3)
                tanh_piece(c, a, 4)
                hidden_high(a, 4)
                tanh_piece(c, a, 5)
                hidden_high(a, 5)
                if isinstance(c.n, int) and c.n == 1:
                    split_early(1)
                exponentials(0)
                exponentials(1)
                tanh_piece(c, a, 6)
                exponentials(2)
                hidden_high(a, 6)
                exponentials(3)
                exponentials(4)
                tanh_piece(c, a, 7)
                exponentials(5)
                sums(0)
                hidden_high(a, 7)
                if o.real:
                    if isinstance(o.n, int) and o.n == 0:
                        act.wait_ge(s["modv_ready"], 4)
                    wait(act, s["t2_done"], o.n + 1)
                    wait(act, s["h2l_ready"], o.n)
                    modulated(h2T, misc[1], 1, o.n, "h2T_ready")
                exponentials(6)
                if o.real:
                    wait(act, s["h2T_ready"], 2 * (o.n + 1))
                    act.activation(h2h[:, :, bass.ds(S * o.n, S)], h2T[:, :, :], ACT.Copy).then_inc(s["h2h_ready"], 1)
                exponentials(7)
                sums(1)
                if o.real:
                    wait(act, s["lsh_ready"], o.n + 1)
                    wait(act, s["rp_ready"], o.n)
                    act.activation(pexp[:, :, :], lsh[:, :, :], ACT.Exp, scale=1.0 / GU_SCALE).then_inc(s["pexp_ready"], 1)

            def split_output_weights():
                act.wait_ge(s["wo_in"], 32)
                act.activation(wo_h[:, :, :], wo32, ACT.Copy, scale=WS).then_inc(s["wsplit_h"], 1)
                act.activation(wr_h[:, :, :], wr32, ACT.Copy, scale=WS).then_inc(s["wsplit_h"], 1)

            def split_early(e):
                act.wait_ge(s["gu_in"], 32 * (e + 1))
                for j in range(IJ):
                    split_gu(e, j)
                split_dn(e, e)

            run_stage_one(act, iteration, {0: lambda: (split_output_weights(), split_early(0))})

            def step(e, blk, par, before, refill_gu=False, refill_dn=False):
                done = IJ * (NB * e + blk)
                for j in range(IJ):
                    wait(act, s["gu_done"], done + j + 1)
                    wait(act, s["sg_ready"], done + j - 1)
                    act.activation(th[j % 2], bank[:, 2 * (j % 2), :], ACT.Tanh, scale=0.5 / GU_SCALE).then_inc(s["th_ready"], 1)
                    wait(act, s["hf_ready"], done + j + 1)
                    act.activation(hid_h[:, par, j, :], hf[j % 2], ACT.Copy).then_inc(s["hidh_ready"], 1)
                    if refill_gu:
                        if j == 0:
                            act.wait_ge(s["gu_in"], 32 * (EARLY + e + 2))
                        split_gu(0, j)
                if refill_dn:
                    wait(act, s["y_done"], BT * NB * e)
                    split_dn(0, EARLY + e)

            run_stage_two(act, step, lambda e, blk, par: None)

        @block.vector
        def _(dve):
            dve.wait_ge(s["tanhc_ready"], 1)
            dve.scalar_tensor_tensor(out=silu_c[:, :, :], in0=tanh_c[:, :, :], scalar=1.0, in1=c32,
                                     op0=ALU.add, op1=ALU.mult).then_inc(s["siluc_ready"], 1)
            def split_gu(place, count, j):
                dve.wait_ge(s["wgu_h"], count)
                dve.scalar_tensor_tensor(out=gu_l[:, place, j, :].rearrange("p (g m) -> p g m", g=2 * KD),
                                         in0=staged_gu[:, :, j * P:(j + 1) * P], scalar=WS,
                                         in1=gu_h[:, place, j, :].rearrange("p (g m) -> p g m", g=2 * KD),
                                         op0=ALU.mult, op1=ALU.subtract).then_inc(s["wgu_l"], 1)

            def split_dn(place, e):
                dve.wait_ge(s["wdn_h"], e + 1)
                dve.scalar_tensor_tensor(out=dn_l[:, place, :, :].rearrange("p j d -> p (j d)"), in0=staged_dn, scalar=WS,
                                         in1=dn_h[:, place, :, :].rearrange("p j d -> p (j d)"),
                                         op0=ALU.mult, op1=ALU.subtract).then_inc(s["wdn_l"], 1)

            def split_expert(place, e):
                for j in range(IJ):
                    split_gu(place, IJ * e + j + 1, j)
                split_dn(place, e)

            def modulation(norm):
                dve.wait_ge(s["mod_done"], norm + 1)
                made = bank[:, 6 - 2 * norm, 0:2 * KD * B].rearrange("p (w n) -> p w n", w=2)
                kept = modv[:, 2 * norm:2 * norm + 2, :, :].rearrange("p w k b -> p w (k b)")
                dve.tensor_scalar(kept[:, 0, :], made[:, 0, :], XS / 2, None, ALU.mult).then_inc(s["modv_ready"], 1)
                dve.tensor_scalar(kept[:, 1, :], made[:, 1, :], XS / 2, XS, ALU.mult, ALU.add).then_inc(s["modv_ready"], 1)

            def modulation_and_weights():
                modulation(0)
                dve.wait_ge(s["bias_in"], 16)
                for first, scale in ((0, QS), (2, XS), (4, XS)):
                    dve.tensor_scalar(bias_s[:, first:first + 2], bias_p[:, first:first + 2], scale, None,
                                      ALU.mult).then_inc(s["bias_s_ready"], 1)
                split_weights(0, wq_l, wq32, wq_h)

            def split_weights(count, lo, full, hi):
                dve.wait_ge(s["wsplit_h"], count + 1)
                dve.scalar_tensor_tensor(out=lo[:, :, :], in0=full, scalar=WS, in1=hi[:, :, :],
                                         op0=ALU.mult, op1=ALU.subtract).then_inc(s["wsplit_l"], 1)

            def gates():
                dve.wait_ge(s["mod_done"], 3)
                rows = bank[0:B, 5, :].rearrange("b (g d) -> b g d", g=2)
                dve.tensor_scalar(gate_r[:, :, :], rows, 0.5, None, ALU.mult).then_inc(s["gr_ready"], 1)
                dve.wait_ge(s["gr_ready"], 1)
                dve.tensor_scalar(gate_s[:, :, :], gate_r[:, :, :], 0.0, 2.0, ALU.is_ge, ALU.mult).then_inc(s["gr_ready"], 1)
                dve.wait_ge(s["gr_ready"], 2)
                dve.scalar_tensor_tensor(out=gate_m[:, :, :], in0=gate_s[:, :, :], scalar=-1.0, in1=gate_r[:, :, :],
                                         op0=ALU.add, op1=ALU.mult).then_inc(s["gr_ready"], 1)
                dve.wait_ge(s["gr_ready"], 3)
                for g, scale in enumerate((1.0, 1.0 / WS)):
                    dve.tensor_scalar(gate_m[:, g, :], gate_m[:, g, :], GATE_MIN, scale, ALU.max, ALU.mult).then_inc(s["gr_ready"], 1)
                dve.wait_ge(s["gr_ready"], 5)
                for g in range(2):
                    dve.scalar_tensor_tensor(out=gate_r[:, g, :], in0=gate_s[:, g, :], scalar=-1.0, in1=gate_m[:, g, :],
                                             op0=ALU.add, op1=ALU.mult).then_inc(s["gates_ready"], 1)
                dve.wait_ge(s["consts_ready"], 2)
                dve.wait_ge(s["bo_in"], 16)

            def statistics(stats, parts, mv, of, src, n):
                stats_sem, halves_sem, parts_sem, mv_sem = (s[f"{name}{of}_ready"] for name in ("st", "halves", "parts", "mv"))
                for t in range(TT):
                    dve.bn_stats(stats[:, t, :], src[:, t, :]).then_inc(stats_sem, 1)
                wait(dve, stats_sem, TT * (n + 1))
                even, odd = stats[:, :, 1:3], stats[:, :, 4:6]
                total, apart, apart2 = parts[:, :, 0:2], parts[:, :, 2], parts[:, :, 3]
                dve.tensor_tensor(total, even, odd, ALU.add).then_inc(halves_sem, 1)
                dve.tensor_tensor(apart, even[:, :, 0], odd[:, :, 0], ALU.subtract).then_inc(halves_sem, 1)
                wait(dve, halves_sem, 2 * (n + 1))
                dve.scalar_tensor_tensor(out=apart2, in0=apart, scalar=0.25, in1=apart, op0=ALU.mult, op1=ALU.mult).then_inc(parts_sem, 1)
                dve.tensor_scalar(mv[:, :, 0], total[:, :, 0], 0.5, None, ALU.mult).then_inc(mv_sem, 1)
                wait(dve, parts_sem, n + 1)
                dve.scalar_tensor_tensor(out=mv[:, :, 1], in0=total[:, :, 1], scalar=1.0 / D, in1=apart2,
                                         op0=ALU.mult, op1=ALU.add).then_inc(mv_sem, 1)

            def normalise(xn, mv, rs, done, src):
                for t in range(TT):
                    dve.tensor_scalar(xn[:, t, :], src[:, t, :], mv[:, t, 0:1], rs[:, t:t + 1], ALU.subtract, ALU.mult).then_inc(s[done], 1)

            def route_logits(o):
                wait(dve, s["rt_done"], o.n + 1)
                logits = bank[:, 6, 0:TT * E].rearrange("p (t e) -> p t e", t=TT)
                dve.tensor_reduce(lmax[:, :], logits, AX.X, ALU.max).then_inc(s["lmax_ready"], 1)
                wait(dve, s["lmax_ready"], o.n + 1)
                dve.tensor_tensor(lsh[:, :, :], logits, lmax[:, :].unsqueeze(2).to_broadcast([P, TT, E]),
                                  ALU.subtract).then_inc(s["lsh_ready"], 1)

            mine = rp[:, :, :].unsqueeze(3).to_broadcast([P, TT, E, E])
            other = rp[:, :, :].unsqueeze(2).to_broadcast([P, TT, E, E])

            def route_sum(a):
                wait(dve, s["pexp_ready"], a.n + 1)
                dve.tensor_reduce(psum_r[:, :], pexp[:, :, :], AX.X, ALU.add).then_inc(s["rsum_ready"], 1)
                wait(dve, s["rsum_ready"], a.n + 1)
                dve.reciprocal(prec[:, :], psum_r[:, :]).then_inc(s["prec_ready"], 1)

            def route_probabilities(a):
                wait(dve, s["prec_ready"], a.n + 1)
                dve.tensor_tensor(rp[:, :, :], pexp[:, :, :], prec[:, :].unsqueeze(2).to_broadcast([P, TT, E]),
                                  ALU.mult).then_inc(s["rp_ready"], 1)

            def route_order(a):
                wait(dve, s["rp_ready"], a.n + 1)
                dve.tensor_tensor(ties[:, :, :, :], other, mine, ALU.is_equal).then_inc(s["ties_ready"], 1)
                dve.tensor_tensor(before[:, :, :, :], other, mine, ALU.is_gt).then_inc(s["before_ready"], 1)
                wait(dve, s["ties_ready"], a.n + 1)
                dve.tensor_tensor(ties[:, :, :, :], ties[:, :, :, :], earlier[:, :, :].unsqueeze(1).to_broadcast([P, TT, E, E]),
                                  ALU.mult).then_inc(s["tied_ready"], 1)

            def route_join(a):
                wait(dve, s["before_ready"], a.n + 1)
                wait(dve, s["tied_ready"], a.n + 1)
                dve.tensor_tensor(before[:, :, :, :], before[:, :, :, :], ties[:, :, :, :], ALU.add).then_inc(s["joined_ready"], 1)

            def route_weigh(a):
                wait(dve, s["joined_ready"], a.n + 1)
                dve.tensor_tensor(ties[:, :, :, :], before[:, :, :, :], other, ALU.mult).then_inc(s["weighed_ready"], 1)

            def route_cumulate(a):
                wait(dve, s["weighed_ready"], a.n + 1)
                dve.tensor_reduce(cum[:, :, :], ties[:, :, :, :], AX.X, ALU.add).then_inc(s["cum_ready"], 1)

            def route_weights(a):
                wait(dve, s["cum_ready"], a.n + 1)
                dve.scalar_tensor_tensor(out=wts[:, bass.ds(TT * a.n, TT), :], in0=cum[:, :, :], scalar=TOP_P, in1=rp[:, :, :],
                                         op0=ALU.is_le, op1=ALU.mult).then_inc(s["w_ready"], 1)

            def gated_piece(c, a, i):
                if a.real:
                    wait(dve, s["the_ready"], CHUNKS * a.n + i + 1)
                    wait(dve, s["hfe_ready"], CHUNKS * a.n + i)
                    dve.scalar_tensor_tensor(out=sg_e[:, :], in0=th_e[:, :], scalar=1.0, in1=bank[:, early_bank(c, i), 0:S],
                                             op0=ALU.add, op1=ALU.mult).then_inc(s["sge_ready"], 1)
                    wait(dve, s["sge_ready"], CHUNKS * a.n + i + 1)
                    wait(dve, s["hidel_ready"], CHUNKS * a.n + i - 1)
                    dve.scalar_tensor_tensor(out=hf_e[:, i % 2, :], in0=sg_e[:, :], scalar=0.5 / GU_SCALE ** 2,
                                             in1=bank[:, early_bank(c, i), S:2 * S], op0=ALU.mult, op1=ALU.mult).then_inc(s["hfe_ready"], 1)

            def early_share(c, a, e):
                if a.real:
                    wait(dve, s["w_ready"], a.n + 1)
                    wait(dve, s["ye_done"], TT * (EARLY * a.n + e + 1))
                    wait(dve, s["acc_ready"], CLEARED + TT * (EARLY * a.n + e))
                    for t in range(TT):
                        tile = acc[:, bass.ds(TT * a.n + t, 1), :].rearrange("p a d -> p (a d)")
                        dve.scalar_tensor_tensor(out=tile, in0=bank[:, down_bank(c, e), t * D:(t + 1) * D],
                                                 scalar=wts[:, bass.ds(TT * a.n + t, 1), e:e + 1].rearrange("p a b -> p (a b)"),
                                                 in1=tile, op0=ALU.mult, op1=ALU.add).then_inc(s["acc_ready"], 1)

            def iteration(c):
                n, o, a, m = c.at(1), c.at(-1), c.at(-2), c.at(2)

                def maxima(c, pair):
                    if not c.real:
                        return
                    wait(dve, s["sc_done"], PAIRS * c.n + pair + 1)
                    if pair == 0:
                        wait(dve, s["nmt_done"], c.n)
                    r = 2 * (pair % 2)
                    dve.tensor_reduce(mx[:, :, :, pair].rearrange("p t o -> p o t"),
                                      bank[:, r:r + 2, :].rearrange("p o (t s) -> p o t s", t=TT),
                                      AX.X, ALU.max).then_inc(s["max_done"], 1)

                def first_late(j):
                    if isinstance(c.n, int) and c.n == B + 1:
                        split_gu(0, IJ * EARLY + j + 1, j)

                def route(*steps):
                    if a.real:
                        for step in steps:
                            step(a)

                route(route_sum)
                gated_piece(c, a, 0)
                route(route_probabilities)
                maxima(c, 2)
                if o.real:
                    wait(dve, s["ta_done"], o.n)
                    for t in range(TT):
                        heads = bank[:, 7 - t, :].rearrange("p (h w) -> p h w", h=H)
                        wait(dve, s["tn_done"], TT * o.n + t + 1)
                        dve.reciprocal(rec[:, t, :], heads[:, :, HD]).then_inc(s["rec_ready"], 1)
                    for t in range(TT):
                        heads = bank[:, 7 - t, :].rearrange("p (h w) -> p h w", h=H)
                        wait(dve, s["rec_ready"], TT * o.n + t + 1)
                        dve.tensor_tensor(at[:, t, :].rearrange("p (h d) -> p h d", h=H), heads[:, :, 0:HD],
                                          rec[:, t, :].unsqueeze(2).to_broadcast([P, H, HD]), ALU.mult).then_inc(s["at_ready"], 1)
                gated_piece(c, a, 1)
                maxima(c, 3)
                maxima(c, 4)
                gated_piece(c, a, 2)
                maxima(c, 5)
                route(route_order)
                gated_piece(c, a, 3)
                maxima(c, 6)
                maxima(c, 7)
                gated_piece(c, a, 4)
                first_late(0)
                route(route_join)
                if c.real:
                    wait(dve, s["nmt_done"], c.n + 1)
                    wait(dve, nm_in[1 - c.par], 32 * (c.at(-1).half + 1))
                    dve.tensor_scalar(nm[:, :], bank[0:H, 7, 0:S], -1.0 / MAXK, None, ALU.mult).then_inc(s["nm_ready"], 1)
                if o.real:
                    wait(dve, s["op_done"], o.n + 1)
                    wait(dve, s["x1_ready"], o.n)
                    dve.scalar_tensor_tensor(out=proj[:, :, :], in0=bank[:, 6, :].rearrange("p (t d) -> p t d", t=TT),
                                             scalar=1.0 / GU_SCALE, in1=bo_bc[:, :].unsqueeze(1).to_broadcast([P, TT, D]),
                                             op0=ALU.mult, op1=ALU.add).then_inc(s["proj_ready"], 1)
                route(route_weigh)
                gated_piece(c, a, 5)
                first_late(1)
                route(route_cumulate)
                if m.real:
                    wait(dve, x_in[m.par], 16 * (m.half + 1))
                    statistics(bn1, parts1, mv1, 1, xa[:, m.par, :, :], m.n)
                route(route_weights)
                if c.real:
                    early_share(c, a, 0)
                if isinstance(c.n, int) and c.n == 1:
                    split_expert(1, 1)
                if o.real:
                    wait(dve, s["x1_ready"], o.n + 1)
                    statistics(bn2, parts2, mv2, 2, xr[:, o.par, :, :], o.n)
                gated_piece(c, a, 6)
                first_late(2)
                if not c.real:
                    gated_piece(c, a, 7)
                    first_late(3)
                if o.real:
                    wait(dve, s["rs2_ready"], o.n + 1)
                    normalise(xn2, mv2, rs2, "xn2_ready", xr[:, o.par, :, :])
                if c.real:
                    gated_piece(c, a, 7)
                else:
                    early_share(c, a, 0)
                if m.real:
                    wait(dve, s["rs1_ready"], m.n + 1)
                    wait(dve, s["t1_done"], m.n)
                    normalise(xn1, mv1, rs1, "xn1_ready", xa[:, m.par, :, :])
                if o.real:
                    wait(dve, s["h2h_ready"], o.n + 1)
                    dve.tensor_tensor(h2l[:, :, bass.ds(S * o.n, S)], h2T[:, :, :], h2h[:, :, bass.ds(S * o.n, S)],
                                      ALU.subtract).then_inc(s["h2l_ready"], 1)
                if isinstance(c.n, int) and c.n == -1:
                    modulation(1)
                    gates()
                    split_weights(1, wo_l, wo32, wo_h)
                    split_weights(2, wr_l, wr32, wr_h)
                    split_expert(0, 0)
                maxima(n, 0)
                if isinstance(c.n, int) and c.n == B + 1:
                    split_dn(0, EARLY)
                early_share(c, a, 1)
                if o.real:
                    route_logits(o)
                maxima(n, 1)

            run_stage_one(dve, iteration, {-1: modulation_and_weights})

            def add_share(e, blk, t):
                done = BT * (NB * e + blk) + t
                wait(dve, s["y_done"], done + 1)
                tile = acc[:, bass.ds(BT * blk + t, 1), :].rearrange("p a d -> p (a d)")
                dve.scalar_tensor_tensor(out=tile, in0=bank[:, 4 + t, 0:D],
                                         scalar=wts[:, bass.ds(BT * blk + t, 1), bass.ds(EARLY + e, 1)].rearrange("p a b -> p (a b)"),
                                         in1=tile, op0=ALU.mult, op1=ALU.add).then_inc(s["acc_ready"], 1)

            def step(e, blk, par, before, refill_gu=False, refill_dn=False):
                done = IJ * (NB * e + blk)
                for j in range(IJ):
                    wait(dve, s["th_ready"], done + j + 1)
                    dve.scalar_tensor_tensor(out=sg[j % 2], in0=th[j % 2], scalar=1.0, in1=bank[:, 2 * (j % 2), :],
                                             op0=ALU.add, op1=ALU.mult).then_inc(s["sg_ready"], 1)
                    wait(dve, s["sg_ready"], done + j + 1)
                    dve.scalar_tensor_tensor(out=hf[j % 2], in0=sg[j % 2], scalar=0.5 / GU_SCALE ** 2,
                                             in1=bank[:, 2 * (j % 2) + 1, :], op0=ALU.mult, op1=ALU.mult).then_inc(s["hf_ready"], 1)
                    wait(dve, s["hidh_ready"], done + j + 1)
                    dve.tensor_tensor(hid_l[:, par, j, :], hf[j % 2], hid_h[:, par, j, :], ALU.subtract).then_inc(s["hidl_ready"], 1)
                    if before is not None and j > 0:
                        add_share(*before, j - 1)
                    if refill_gu:
                        split_gu(0, IJ * (EARLY + e + 1) + j + 1, j)
                if before is not None:
                    add_share(*before, IJ - 1)
                if refill_dn:
                    split_dn(0, EARLY + e)

            def drain(e, blk, par):
                dve.wait_ge(s["last_in"], 32)
                for t in range(BT):
                    add_share(e, blk, t)
                    tile = acc[:, BT * blk + t, :]
                    wait(dve, s["acc_ready"], CLEARED + NT * (E - 1) + BT * blk + t + 1)
                    dve.tensor_tensor(tile, tile, gbl[:, t // TT, :], ALU.mult).then_inc(s["last_mul"], 1)
                    wait(dve, s["last_mul"], t + 1)
                    dve.tensor_tensor(tile, tile, x1l[:, t, :], ALU.add).then_inc(s["last_add"], 1)

            run_stage_two(dve, step, drain)

        @block.tensor
        def _(pe):
            def modulation(norm):
                for q in range(2):
                    for m in range(KD):
                        at_col = (q * KD + m) * B
                        col = (3 * norm + q) * D + m * P
                        for k in range(KD):
                            mm = pe.matmul(bank[:, 6 - 2 * norm, at_col:at_col + B], wmod32[:, k, col:col + P],
                                           silu_c[:, k, :], start=(k == 0), stop=(k == KD - 1))
                mm.then_inc(s["mod_done"], 1)

            def gates():
                for g, col in enumerate((2, 5)):
                    for k in range(KD):
                        mm = pe.matmul(bank[0:B, 5, g * D:(g + 1) * D], silu_c[:, k, :], wmod32[:, k, col * D:(col + 1) * D],
                                       start=(k == 0), stop=(k == KD - 1))
                mm.then_inc(s["mod_done"], 1)

            pe.wait_ge(s["siluc_ready"], 1)
            pe.wait_ge(s["wmod_in"], 16)
            modulation(0)
            pe.wait_ge(s["ident_ready"], 2)
            pe.wait_ge(s["modv_ready"], 2)

            def product(dst, weights, moving, pieces):
                terms = [pair for k in range(pieces) for pair in passes(*weights(k), *moving(k))]
                for i, (w, a) in enumerate(terms):
                    mm = pe.matmul(dst, w, a, start=(i == 0), stop=(i == len(terms) - 1))
                return mm

            def iteration(c):
                n, o, a = c.at(1), c.at(-1), c.at(-2)

                def gate_up_piece(i):
                    if a.real:
                        e, j = i // IJ, i % IJ
                        wait(pe, s["wgu_l"], i + 1)
                        if i == 0:
                            wait(pe, s["h2h_ready"], a.n + 1)
                            wait(pe, s["h2l_ready"], a.n + 1)
                        spare = early_bank(c, i) != 5
                        wait(pe, s["hfe_ready"], CHUNKS * a.n + i - (0 if c.real or i == 0 else 1))
                        if spare:
                            wait(pe, s["exp_done"], PAIRS * B)
                        elif i == 0 and not o.real:
                            wait(pe, s["acc_ready"], CLEARED + TT * EARLY * a.n)
                        tokens = bass.ds(S * a.n, S)
                        for g in range(2):
                            mm = product(bank[:, early_bank(c, i), g * S:(g + 1) * S],
                                         lambda k: (gu_h[:, e, j, (g * KD + k) * P:(g * KD + k + 1) * P],
                                                    gu_l[:, e, j, (g * KD + k) * P:(g * KD + k + 1) * P]),
                                         lambda k: (h2h[:, k, tokens], h2l[:, k, tokens]), KD)
                        mm.then_inc(s["gue_done"], 1)

                def early_down(e, t):
                    if a.real:
                        if t == 0:
                            wait(pe, s["wdn_l"], e + 1)
                            wait(pe, s["hidel_ready"], CHUNKS * a.n + IJ * (e + 1))
                            if not c.real:
                                wait(pe, s["au_ready"], 2 * B)
                            elif e > 0 and o.real:
                                wait(pe, s["h2T_ready"], 2 * (o.n + 1))
                            else:
                                wait(pe, s["nm_ready"], c.n + 1)
                            wait(pe, s["acc_ready"], CLEARED + TT * (EARLY * a.n + (e if c.real else 0)))
                        mm = product(bank[:, down_bank(c, e), t * D:(t + 1) * D],
                                     lambda j: (hid_eh[:, e, j, t * P:(t + 1) * P], hid_el[:, e, j, t * P:(t + 1) * P]),
                                     lambda j: (dn_h[:, e, j, :], dn_l[:, e, j, :]), IJ)
                        mm.then_inc(s["ye_done"], 1)

                def scores(c, pair):
                    if not c.real:
                        return
                    if pair == 0:
                        wait(pe, stack_in[c.par], 12 * 16 * (c.half + 1))
                    if pair < 2:
                        wait(pe, s["exp_done"], PAIRS * c.n - 1 + pair)
                    else:
                        wait(pe, s["max_done"], PAIRS * c.n + pair - 1)
                    for t in range(TT):
                        for odd in range(2):
                            rows = slice(64 * odd, 64 * odd + STACK)
                            mm = pe.matmul(bank[:, 2 * (pair % 2) + odd, t * S:(t + 1) * S],
                                           qst[rows, c.par, pair, t * P:(t + 1) * P], kst[rows, c.par, pair, :],
                                           start=True, stop=True)
                    mm.then_inc(s["sc_done"], 1)

                def scores_transposed(pair):
                    if not c.real:
                        return
                    if pair == 0:
                        wait(pe, nm_in[c.par], 32 * (c.half + 1))
                    if pair < 2:
                        wait(pe, s["max_done"], PAIRS * c.n + PAIRS - 1 + pair)
                    else:
                        wait(pe, s["exp_done"], PAIRS * c.n + pair - 1)
                    for t in range(TT):
                        for odd in range(2):
                            rows = slice(64 * odd, 64 * odd + STACK + 1)
                            mm = pe.matmul(bank[:, 2 * (pair % 2) + odd, t * S:(t + 1) * S],
                                           kst[rows, c.par, pair, t * P:(t + 1) * P], qst[rows, c.par, pair, :],
                                           start=True, stop=True)
                    mm.then_inc(s["scT_done"], 1)

                def weighted_values(group):
                    if not c.real:
                        return
                    wait(pe, s["exp_done"], PAIRS * c.n + 2 * (group + 1))
                    if group == 0:
                        wait(pe, s["v_ready"], TT * (c.n + 1))
                    if group % 2 == 0:
                        wait(pe, s["au_ready"], 2 * c.n + group // 2)
                    for t in range(TT):
                        for i in range(4):
                            mm = pe.matmul(bank[VW * i:VW * (i + 1), 4, (group % 2) * S:(group % 2 + 1) * S],
                                           vx[:, c.par, t, 4 * group + i, :], prob[:, group % 2, i, t, :],
                                           start=(t == 0), stop=(t == TT - 1), skip_group_check=True,
                                           tile_position=(0, VW * i))
                    mm.then_inc(s["pv_done"], 1)

                def transpose_tiles(which, src, done):
                    for k in range(KD):
                        for t in range(TT):
                            mm = pe.transpose(bank[:, which, k * S + t * P:k * S + (t + 1) * P], src[:, t, k * P:(k + 1) * P], ident[:, :])
                    mm.then_inc(s[done], 1)

                def ln1_transposed():
                    if n.real:
                        if isinstance(c.n, int) and c.n < 2:
                            wait(pe, s["v_ready"], TT * n.n)
                        wait(pe, s["lsh_ready"], c.n - 1)
                        wait(pe, s["xn1_ready"], TT * (n.n + 1))
                        transpose_tiles(6, xn1, "t1_done")

                def attention_by_token(t):
                    if o.real:
                        if t == 0:
                            wait(pe, s["au_ready"], 2 * (o.n + 1))
                            wait(pe, s["h2T_ready"], 2 * o.n)
                            if c.at(-3).real:
                                wait(pe, s["acc_ready"], CLEARED + TT * EARLY * (c.n - 2))
                        elif n.real:
                            wait(pe, s["hT_ready"], 2 * (n.n + 1))
                        else:
                            wait(pe, s["lsh_ready"], o.n)
                        for g in range(4):
                            mm = pe.transpose(bank[:, 7 - t, g * P:(g + 1) * P], au[:, g, t * P:(t + 1) * P], ident[:, :])
                        mm.then_inc(s["tn_done"], 1)

                def q_or_k(which):
                    if n.real:
                        done, piece = (("qp_done", 0), ("kp_done", 2))[which]
                        wait(pe, s["hh_ready"], n.n + 1)
                        wait(pe, s["hl_ready"], n.n + 1)
                        if isinstance(n.n, int) and n.n == 0:
                            wait(pe, s["wsplit_l"], 1)
                        if o.real:
                            wait(pe, s["at_ready"], TT * o.n + which + 1)
                        elif which == 0:
                            wait(pe, s["q32_ready"], 2 * n.n)
                        else:
                            wait(pe, s["hT_ready"], 2 * (n.n + 1))
                        for m in range(2):
                            cols = slice((piece + m) * P, (piece + m + 1) * P)
                            mm = product(bank[:, 7 - which, m * S:(m + 1) * S],
                                         lambda k: (wq_h[:, k, cols], wq_l[:, k, cols]),
                                         lambda k: (hh[:, k, :], hl[:, k, :]), KD)
                        mm.then_inc(s[done], 1)

                def attention_transposed():
                    if o.real:
                        wait(pe, s["at_ready"], TT * (o.n + 1))
                        if n.real:
                            wait(pe, s["q32_ready"], 2 * (n.n + 1))
                        transpose_tiles(7, at, "ta_done")

                def v():
                    if n.real:
                        wait(pe, s["k32_ready"], 2 * (n.n + 1))
                        for t in range(TT):
                            mm = product(bank[:, 6, t * D:(t + 1) * D],
                                         lambda k: (hh[:, k, t * P:(t + 1) * P], hl[:, k, t * P:(t + 1) * P]),
                                         lambda k: (wq_h[:, k, 2 * D:3 * D], wq_l[:, k, 2 * D:3 * D]), KD)
                        mm.then_inc(s["vp_done"], 1)

                def maxima_transposed():
                    if c.real:
                        wait(pe, s["max_done"], PAIRS * (c.n + 1))
                        if o.real:
                            wait(pe, s["aT_ready"], 2 * (o.n + 1))
                        elif n.real:
                            wait(pe, s["q32_ready"], 2 * (n.n + 1))
                        for t in range(TT):
                            mm = pe.transpose(bank[0:H, 7, t * P:(t + 1) * P],
                                              mx[:, t, :, :].rearrange("p o s -> p (o s)"), ident[:, :])
                        mm.then_inc(s["nmt_done"], 1)

                def output_projection():
                    if o.real:
                        if isinstance(o.n, int) and o.n == 0:
                            wait(pe, s["wsplit_l"], 3)
                        wait(pe, s["ah_ready"], o.n + 1)
                        wait(pe, s["al_ready"], o.n + 1)
                        if n.real:
                            wait(pe, s["v_ready"], TT * (n.n + 1))
                        for t in range(TT):
                            mm = product(bank[:, 6, t * D:(t + 1) * D],
                                         lambda k: (ah[:, k, t * P:(t + 1) * P], al[:, k, t * P:(t + 1) * P]),
                                         lambda k: (wo_h[:, k, :], wo_l[:, k, :]), KD)
                        mm.then_inc(s["op_done"], 1)

                def ln2_transposed():
                    if o.real:
                        wait(pe, s["xn2_ready"], TT * (o.n + 1))
                        if c.real:
                            wait(pe, s["nm_ready"], c.n + 1)
                        if c.real and a.real:
                            wait(pe, s["acc_ready"], CLEARED + TT * (EARLY * a.n + 1))
                        transpose_tiles(7, xn2, "t2_done")

                def router():
                    if o.real:
                        wait(pe, s["h2h_ready"], o.n + 1)
                        wait(pe, s["h2l_ready"], o.n + 1)
                        for t in range(TT):
                            tokens = bass.ds(S * o.n + t * P, P)
                            mm = product(bank[:, 6, t * E:(t + 1) * E],
                                         lambda k: (h2h[:, k, tokens], h2l[:, k, tokens]),
                                         lambda k: (wr_h[:, k, :], wr_l[:, k, :]), KD)
                        mm.then_inc(s["rt_done"], 1)

                gate_up_piece(0)
                ln1_transposed()
                scores(c, 2)
                attention_by_token(0)
                scores(c, 3)
                attention_by_token(1)
                gate_up_piece(1)
                scores(c, 4)
                q_or_k(0)
                gate_up_piece(2)
                scores(c, 5)
                q_or_k(1)
                attention_transposed()
                gate_up_piece(3)
                scores(c, 6)
                v()
                scores(c, 7)
                gate_up_piece(4)
                output_projection()
                maxima_transposed()
                gate_up_piece(5)
                if not c.real and a.real:
                    gate_up_piece(6)
                    gate_up_piece(7)
                    early_down(0, 0)
                    early_down(0, 1)
                    ln2_transposed()
                    early_down(1, 0)
                    early_down(1, 1)
                    router()
                    return
                early_down(0, 0)
                early_down(0, 1)
                scores_transposed(0)
                scores_transposed(1)
                gate_up_piece(6)
                scores_transposed(2)
                weighted_values(0)
                scores_transposed(3)
                scores_transposed(4)
                gate_up_piece(7)
                scores_transposed(5)
                weighted_values(1)
                ln2_transposed()
                scores_transposed(6)
                weighted_values(2)
                scores_transposed(7)
                if isinstance(c.n, int) and c.n == -1:
                    wait(pe, s["wmod_rest_in"], 16)
                    modulation(1)
                    gates()
                early_down(1, 0)
                scores(n, 0)
                early_down(1, 1)
                router()
                weighted_values(3)
                scores(n, 1)

            run_stage_one(pe, iteration)

            def gate_up(e, blk, j, first):
                done = IJ * (NB * e + blk)
                if first:
                    wait(pe, s["wgu_l"], IJ * (EARLY + e) + j + 1)
                wait(pe, s["hf_ready"], done + j - 1)
                tokens = bass.ds(TB * blk, TB)
                for g in range(2):
                    mm = product(bank[:, 2 * (j % 2) + g, :],
                                 lambda k: (gu_h[:, 0, j, (g * KD + k) * P:(g * KD + k + 1) * P],
                                            gu_l[:, 0, j, (g * KD + k) * P:(g * KD + k + 1) * P]),
                                 lambda k: (h2h[:, k, tokens], h2l[:, k, tokens]), KD)
                mm.then_inc(s["gu_done"], 1)

            def down(e, blk, par, t):
                done = BT * (NB * e + blk)
                if t == 0:
                    wait(pe, s["wdn_l"], EARLY + e + 1)
                    wait(pe, s["hidl_ready"], IJ * (NB * e + blk + 1))
                wait(pe, s["acc_ready"], CLEARED + NT * EARLY + done + t + 1 - BT)
                mm = product(bank[:, 4 + t, 0:D],
                             lambda j: (hid_h[:, par, j, t * P:(t + 1) * P], hid_l[:, par, j, t * P:(t + 1) * P]),
                             lambda j: (dn_h[:, 0, j, :], dn_l[:, 0, j, :]), IJ)
                mm.then_inc(s["y_done"], 1)

            def step(e, blk, par, before, refill_gu=False, refill_dn=False):
                for j in range(IJ):
                    gate_up(e, blk, j, first=(before is None or refill_dn))
                    if before is not None and j > 0:
                        down(*before, 1 - par, j - 1)
                if before is not None:
                    down(*before, 1 - par, IJ - 1)
                if before is None:
                    pe.wait_ge(s["lsh_ready"], B)
                    pe.wait_ge(s["acc_ready"], CLEARED + NT * EARLY)

            def drain(e, blk, par):
                for t in range(BT):
                    down(e, blk, par, t)

            pe.wait_ge(s["hfe_ready"], CHUNKS * B)
            run_stage_two(pe, step, drain)


def kernel(**inputs):
    import numpy as np
    import concourse.bacc as bacc
    from concourse.bass_utils import run_bass_kernel_spmd

    t = lambda name: np.asarray(inputs[name])
    arrays = {
        "x": t("L0_attn_x"),
        "wqkv_t": t("L0_attn_w_qkv").T,
        "bqkv_p": t("L0_attn_b_qkv").reshape(6, P).T,
        "wo_t": t("L0_attn_w_o").T,
        "b_o": t("L0_attn_b_o"),
        "router_t": t("L0_ffn_router_w").T,
        "gate_t": t("L0_ffn_gate_w").transpose(0, 2, 1),
        "up_t": t("L0_ffn_up_w").transpose(0, 2, 1),
        "down_t": t("L0_ffn_down_w").transpose(0, 2, 1),
        "c_t": t("L0_c").T,
        "wmod": t("L0_wmod"),
    }
    arrays = {f"in_{k}": np.ascontiguousarray(v) for k, v in arrays.items()}
    nc = bacc.Bacc("TRN2", target_bir_lowering=False, num_devices=1)
    args = [nc.dram_tensor(k, v.shape, mybir.dt.from_np(v.dtype), kind="ExternalInput").ap() for k, v in arrays.items()]
    out = nc.dram_tensor("out", (B, S, D), F32, kind="ExternalOutput").ap()
    adaln_block(nc, *args, out)
    r = run_bass_kernel_spmd(nc, [arrays], core_ids=[0])
    return r.results[0]["out"]
```
